# Optimizing a Trainium2 kernel written in Bass

```python
import numpy as np
import jax
import jax.numpy as jnp

def _softmax(x, axis=-1):
    return jax.nn.softmax(x, axis=axis)

def _gelu(x):
    return jax.nn.gelu(x, approximate=True)

def _silu(x):
    return jax.nn.silu(x)

def _sigmoid(x):
    return jax.nn.sigmoid(x)

def _layernorm(x, axis=-1, eps=1e-05):
    m = jnp.mean(x, axis=axis, keepdims=True)
    v = jnp.var(x, axis=axis, keepdims=True)
    return (x - m) / jnp.sqrt(v + eps)

def _scatter_add(tgt, idx, src, axis=0):
    return tgt.at[idx].add(src)

def _segment_sum(src, seg, n):
    return jax.ops.segment_sum(src, seg, n)
kernel_name = 'mk_flamingo_gated_d1_seqx_r8_f135c0'

def setup_inputs(seed: int=0):
    np.random.seed(seed)
    _w = jnp.asarray

    def _rec_inputs():
        import jax
        import jax.numpy as jnp
        _rk = jax.random.key(seed)
        x = 4.136e-05 + 0.9999 * jax.random.normal(jax.random.fold_in(_rk, 1), (4, 256, 256), jnp.float32)
        _lenS = 256 - jax.random.randint(jax.random.fold_in(_rk, 7), (4,), 0, max(1, 256 // 4) + 1, jnp.int32)
        _lenS2 = 256 - jax.random.randint(jax.random.fold_in(_rk, 8), (4,), 0, max(1, 256 // 4) + 1, jnp.int32)
        _ctx_1024P = jax.random.normal(jax.random.fold_in(_rk, 11), (4, 16, 128), jnp.float32)
        _ctx_1024c = jax.random.dirichlet(jax.random.fold_in(_rk, 511), 0.3 * jnp.ones((16,), jnp.float32), (4, 256))
        _ctx_1024t = jnp.einsum('bsk,bkd->bsd', _ctx_1024c, _ctx_1024P)
        _ctx_1024t = _ctx_1024t * jax.lax.rsqrt(jnp.mean(jnp.square(_ctx_1024t)) + 1e-12) * 0.953939
        ctx_1024 = -0.000292821 + 1.00034 * (_ctx_1024t + 0.3 * jax.random.normal(jax.random.fold_in(_rk, 611), (4, 256, 128), jnp.float32))
        _g = jax.random.normal(jax.random.fold_in(_rk, 9001), (2, 1), jnp.float32)
        _g = jnp.sign(_g) * jnp.maximum(jnp.abs(_g), 1.0) + (_g == 0) * 1.0
        g_xattn = _g[0]
        g_ffn = _g[1]
        return (x, ctx_1024, g_xattn, g_ffn)
    x, ctx_1024, g_xattn, g_ffn = _rec_inputs()

    def _L0_xattn_setup():
        import jax, jax.numpy as jnp
        import numpy as np
        import math
        B, L, DM = (2, 256, 128)
        DS, DC, EXP = (16, 4, 2)
        DI = EXP * DM
        DR = math.ceil(DM / 16)
        DT_MIN, DT_MAX, DT_FLOOR = (0.001, 0.1, 0.0001)

        def _ssm_forward(hidden_states, z, in_proj_w, conv_w, conv_b, x_proj_w, dt_proj_w, dt_proj_b, A_log, D):
            b = hidden_states.shape[0]
            x = jnp.einsum('ed,bld->bel', in_proj_w, hidden_states)
            xp = jnp.pad(x, ((0, 0), (0, 0), (DC - 1, 0)))
            xc = jax.lax.conv_general_dilated(xp, conv_w[:, None, :], window_strides=(1,), padding='VALID', dimension_numbers=('NCH', 'OIH', 'NCH'), feature_group_count=DI)
            u = jax.nn.silu(xc + conv_b[None, :, None])
            x_dbl = jnp.einsum('ke,bel->bkl', x_proj_w, u)
            dt_lo = x_dbl[:, :DR]
            Bm = x_dbl[:, DR:DR + DS]
            Cm = x_dbl[:, DR + DS:]
            delta = jax.nn.softplus(jnp.einsum('er,brl->bel', dt_proj_w, dt_lo) + dt_proj_b[None, :, None])
            A = -jnp.exp(A_log)

            def step(state, xs):
                d_t, B_t, C_t, u_t = xs
                dA = jnp.exp(d_t[..., None] * A)
                state = state * dA + (d_t * u_t)[..., None] * B_t[:, None, :]
                y_t = jnp.einsum('ben,bn->be', state, C_t)
                return (state, y_t)
            xs = (jnp.moveaxis(delta, -1, 0), jnp.moveaxis(Bm, -1, 0), jnp.moveaxis(Cm, -1, 0), jnp.moveaxis(u, -1, 0))
            state0 = jnp.zeros((b, DI, DS), delta.dtype)
            _, ys = jax.lax.scan(step, state0, xs)
            y = jnp.moveaxis(ys, 0, -1)
            y = y + D[None, :, None] * u
            y = y * jax.nn.silu(z)
            return jnp.swapaxes(y, 1, 2)
        key = jax.random.key(seed)
        ks = jax.random.split(key, 8)
        hidden_states = jax.random.normal(ks[0], (B, L, DM), jnp.float32)
        z = jax.random.normal(ks[1], (B, DI, L), jnp.float32)
        in_proj_w = jax.random.normal(ks[2], (DI, DM), jnp.float32) * DM ** (-0.5)
        conv_w = jax.random.normal(ks[3], (DI, DC), jnp.float32) * DC ** (-0.5)
        conv_b = jnp.zeros((DI,), jnp.float32)
        x_proj_w = jax.random.normal(ks[4], (DR + 2 * DS, DI), jnp.float32) * DI ** (-0.5)
        dt_std = DR ** (-0.5)
        dt_proj_w = jax.random.uniform(ks[5], (DI, DR), jnp.float32, -dt_std, dt_std)
        dt = jnp.exp(jax.random.uniform(ks[6], (DI,), jnp.float32) * (math.log(DT_MAX) - math.log(DT_MIN)) + math.log(DT_MIN))
        dt = jnp.clip(dt, DT_FLOOR)
        dt_proj_b = dt + jnp.log(-jnp.expm1(-dt))
        A_log = jnp.log(jnp.broadcast_to(jnp.arange(1, DS + 1, dtype=jnp.float32), (DI, DS)))
        D = jnp.ones((DI,), jnp.float32)
        return dict(hidden_states=hidden_states, z=z, in_proj_w=in_proj_w, conv_w=conv_w, conv_b=conv_b, x_proj_w=x_proj_w, dt_proj_w=dt_proj_w, dt_proj_b=dt_proj_b, A_log=A_log, D=D)
    _L0_xattn_all = _L0_xattn_setup()
    _L0_xattn_in = {k: v for k, v in _L0_xattn_all.items() if k in ('in_proj_w', 'conv_w', 'conv_b', 'x_proj_w', 'dt_proj_w', 'dt_proj_b', 'A_log', 'D')}
    del _L0_xattn_all

    def _L0_ffn_setup():
        import jax, jax.numpy as jnp
        import numpy as np

        def _sparsify_2to4(h):
            B, S, I = h.shape
            g = h.reshape(B, S, I // 4, 4)
            a = jnp.abs(g)
            _, idx = jax.lax.top_k(a, 2)
            pos = jnp.arange(4)
            mask = (pos == idx[..., 0:1]) | (pos == idx[..., 1:2])
            return (g * mask.astype(g.dtype)).reshape(B, S, I)
        key = jax.random.key(seed)
        k1, k2, k3, k4 = jax.random.split(key, 4)
        B, S, H, I = (4, 256, 256, 1024)
        x = jax.random.normal(k1, (B, S, H), dtype=jnp.float32)
        w_gate = jax.random.normal(k2, (H, I), dtype=jnp.float32) / np.sqrt(H)
        w_up = jax.random.normal(k3, (H, I), dtype=jnp.float32) / np.sqrt(H)
        w_down = jax.random.normal(k4, (I, H), dtype=jnp.float32) / np.sqrt(I)
        return {'x': x, 'w_gate': w_gate, 'w_up': w_up, 'w_down': w_down}
    _L0_ffn_all = _L0_ffn_setup()
    _L0_ffn_in = {k: v for k, v in _L0_ffn_all.items() if k in ('w_gate', 'w_up', 'w_down')}
    del _L0_ffn_all
    return {'x': x, 'ctx_1024': ctx_1024, 'g_xattn': g_xattn, 'g_ffn': g_ffn, 'L0_xattn_in_proj_w': _L0_xattn_in['in_proj_w'], 'L0_xattn_conv_w': _L0_xattn_in['conv_w'], 'L0_xattn_conv_b': _L0_xattn_in['conv_b'], 'L0_xattn_x_proj_w': _L0_xattn_in['x_proj_w'], 'L0_xattn_dt_proj_w': _L0_xattn_in['dt_proj_w'], 'L0_xattn_dt_proj_b': _L0_xattn_in['dt_proj_b'], 'L0_xattn_A_log': _L0_xattn_in['A_log'], 'L0_xattn_D': _L0_xattn_in['D'], 'L0_ffn_w_gate': _L0_ffn_in['w_gate'], 'L0_ffn_w_up': _L0_ffn_in['w_up'], 'L0_ffn_w_down': _L0_ffn_in['w_down']}

def reference(x, ctx_1024, g_xattn, g_ffn, L0_xattn_in_proj_w, L0_xattn_conv_w, L0_xattn_conv_b, L0_xattn_x_proj_w, L0_xattn_dt_proj_w, L0_xattn_dt_proj_b, L0_xattn_A_log, L0_xattn_D, L0_ffn_w_gate, L0_ffn_w_up, L0_ffn_w_down):
    import jax
    import jax.numpy as jnp

    def _L0_xattn_ref(hidden_states, z, in_proj_w, conv_w, conv_b, x_proj_w, dt_proj_w, dt_proj_b, A_log, D):
        import jax, jax.numpy as jnp
        import numpy as np
        import math
        B, L, DM = (2, 256, 128)
        DS, DC, EXP = (16, 4, 2)
        DI = EXP * DM
        DR = math.ceil(DM / 16)
        DT_MIN, DT_MAX, DT_FLOOR = (0.001, 0.1, 0.0001)

        def _ssm_forward(hidden_states, z, in_proj_w, conv_w, conv_b, x_proj_w, dt_proj_w, dt_proj_b, A_log, D):
            b = hidden_states.shape[0]
            x = jnp.einsum('ed,bld->bel', in_proj_w, hidden_states)
            xp = jnp.pad(x, ((0, 0), (0, 0), (DC - 1, 0)))
            xc = jax.lax.conv_general_dilated(xp, conv_w[:, None, :], window_strides=(1,), padding='VALID', dimension_numbers=('NCH', 'OIH', 'NCH'), feature_group_count=DI)
            u = jax.nn.silu(xc + conv_b[None, :, None])
            x_dbl = jnp.einsum('ke,bel->bkl', x_proj_w, u)
            dt_lo = x_dbl[:, :DR]
            Bm = x_dbl[:, DR:DR + DS]
            Cm = x_dbl[:, DR + DS:]
            delta = jax.nn.softplus(jnp.einsum('er,brl->bel', dt_proj_w, dt_lo) + dt_proj_b[None, :, None])
            A = -jnp.exp(A_log)

            def step(state, xs):
                d_t, B_t, C_t, u_t = xs
                dA = jnp.exp(d_t[..., None] * A)
                state = state * dA + (d_t * u_t)[..., None] * B_t[:, None, :]
                y_t = jnp.einsum('ben,bn->be', state, C_t)
                return (state, y_t)
            xs = (jnp.moveaxis(delta, -1, 0), jnp.moveaxis(Bm, -1, 0), jnp.moveaxis(Cm, -1, 0), jnp.moveaxis(u, -1, 0))
            state0 = jnp.zeros((b, DI, DS), delta.dtype)
            _, ys = jax.lax.scan(step, state0, xs)
            y = jnp.moveaxis(ys, 0, -1)
            y = y + D[None, :, None] * u
            y = y * jax.nn.silu(z)
            return jnp.swapaxes(y, 1, 2)
        return _ssm_forward(hidden_states, z, in_proj_w, conv_w, conv_b, x_proj_w, dt_proj_w, dt_proj_b, A_log, D)

    def _L0_ffn_ref(x, w_gate, w_up, w_down):
        import jax, jax.numpy as jnp
        import numpy as np

        def _sparsify_2to4(h):
            B, S, I = h.shape
            g = h.reshape(B, S, I // 4, 4)
            a = jnp.abs(g)
            _, idx = jax.lax.top_k(a, 2)
            pos = jnp.arange(4)
            mask = (pos == idx[..., 0:1]) | (pos == idx[..., 1:2])
            return (g * mask.astype(g.dtype)).reshape(B, S, I)
        h = jax.nn.silu(jnp.einsum('bsh,hi->bsi', x, w_gate)) * jnp.einsum('bsh,hi->bsi', x, w_up)
        h_sparse = _sparsify_2to4(h)
        return jnp.einsum('bsi,ih->bsh', h_sparse, w_down)
    x = x + jnp.tanh(g_xattn[0]) * _L0_xattn_ref(ctx_1024, _layernorm(x, axis=-1), L0_xattn_in_proj_w, L0_xattn_conv_w, L0_xattn_conv_b, L0_xattn_x_proj_w, L0_xattn_dt_proj_w, L0_xattn_dt_proj_b, L0_xattn_A_log, L0_xattn_D)
    x = x + jnp.tanh(g_ffn[0]) * _L0_ffn_ref(_layernorm(x, axis=-1), L0_ffn_w_gate, L0_ffn_w_up, L0_ffn_w_down)
    return x

_drawn_inputs = setup_inputs


def setup_inputs(seed=0):
    import zlib

    import numpy as np

    out = dict(_drawn_inputs(seed))
    spreads = {'L0_xattn_conv_b': (0.0, 0.1), 'L0_xattn_D': (1.0, 0.2)}
    factors = {'L0_xattn_dt_proj_w': 4.476}
    for name, (base, spread) in spreads.items():
        noise = np.random.default_rng([zlib.crc32(name.encode()), seed]).standard_normal(out[name].shape)
        drawn = base * np.exp(spread * noise) if base else spread * noise
        out[name] = jnp.asarray(drawn.astype(out[name].dtype))
    for name, factor in factors.items():
        out[name] = (out[name] * factor).astype(out[name].dtype)
    return out
```

```python
from contextlib import ExitStack

import concourse.bass as bass
from concourse import mybir

B, L, D_CTX, D_IN, NS, DR, TAPS, HID = 4, 256, 128, 256, 16, 8, 4, 1024
P = 128
C = D_IN // P
ES = P // NS
GROUPS = D_IN // ES
UNITS = GROUPS // 2
QUADS = 4
SETS = GROUPS // C // QUADS
KB = D_IN // P
IC = HID // (4 * P)
EPS = 1e-5

N_DECAY = 6
N_STATE = 4
N_PROD = 6
SPREAD_AHEAD = 4


T, A, V, G = "tensor", "scalar", "vector", "gpsimd"
ALL = (T, A, V, G)


def order():
    steps = [(ALL, s) for s in (
        [("load",), ("masks",), ("taps",), ("project",), ("context", 0)] + [("conv", 0, q) for q in range(4)]
        + [("gate_in", 0), ("bc", 0), ("tables",), ("step_low", 0), ("step", 0), ("softplus", 0), ("delta", 0),
           ("halves", 0, 0), ("halves", 0, 1), ("context", 1), ("ahead",)])]
    at = {n: [] for n in range(B * UNITS)}
    late = []

    def put(n, engines, *step):
        (at[n] if n < B * UNITS else late).append((engines, step))

    for b in range(B):
        first = UNITS * b

        n = first - UNITS
        if b >= 1:
            if b >= 2:
                put(n - 2, ALL, "context", b)
            for q in range(4):
                put(n + q, (T,), "conv", b, q)
            put(n + 4, (A,), "gate_in", b)
            put(n + 5, (T,), "bc", b)
            put(n + 6, (A,), "bc", b)
            put(n + 6, (T, A), "step_low", b)
            put(n + 7, (T, A), "step", b)
            put(n + 7, (A,), "softplus", b)
            put(n + 8, (G, V), "softplus", b)
            put(n + 9, (V, G), "delta", b)
            put(n + 10, (A, V), "halves", b, 0)
            put(n + 11, (A, V), "halves", b, 1)
        if b == 0:
            for i in range(4):
                put(i, (A, G), "split_up", i)

        n = first + UNITS
        put(first + 11, (V,), "finish", b, 0)
        if b < B - 1:
            put(n + 3, (V,), "finish", b, 1)
            put(n + 4, (T,), "residual", b)
            put(n + 5, (V, G), "residual", b)
            put(n + 6, (V,), "norm", b)
            put(n + 7, (T, A), "normed", b)
            put(n + 8, (V,), "normed", b)
            put(n + 8, (T,), "gate", b, 0)
            put(n + 9, (T,), "gate", b, 1)
            put(n + 10, (A,), "gate", b, 0)
            put(n + 10, (A,), "gate", b, 1)
            put(n + 10, (T, A), "gate", b, 2)
            put(n + 10, (T, A), "gate", b, 3)
            for i in range(4):
                put(n + 11 + i, (T,), "up", b, i)
                put(n + 12 + i, (V,), "up", b, i)
            for c in range(IC):
                k = n + 13 + 3 * c
                put(k, (A,), "compare", b, c)
                put(k + 1, (V,), "compare", b, c)
                put(k + 2, (T,), "wins", b, c, 0)
                put(k + 2 + (c == 0), (T,), "wins", b, c, 1)
                put(k + 3, (V,), "wins", b, c, 0)
                put(k + 3 + (c == 0), (V,), "wins", b, c, 1)
            for i in range(3):
                put(n + 20 + i, (T,), "down", b, i)
            put(n + 23, (V,), "down", b, 2)
            for i in range(3):
                put(n + 25 + 2 * i, (T,), "down", b, 3 + i)
            put(n + 30, (V,), "down", b, 5)
    for n in range(B * UNITS):
        steps.append((ALL, ("unit", n // UNITS, n % UNITS)))
        steps += at[n]
    last = B - 1
    steps += late[:8] + [(ALL, s) for s in [("flush",), ("finish", last, 1), ("residual", last), ("norm", last)]]
    late = late[8:]
    steps += late
    steps += [(ALL, s) for s in (
        [("normed", last)]
        + [("gate", last, i) for i in range(2)] + [("up", last, i) for i in range(2)] + [("compare", last, 0)]
        + [("gate", last, i) for i in range(2, 4)] + [("up", last, i) for i in range(2, 4)]
        + [("wins", last, 0, 0), ("wins", last, 0, 1), ("compare", last, 1)]
        + [("wins", last, 1, 0), ("wins", last, 1, 1)] + [("down", last, k) for k in range(6)])]
    return steps


def banks(steps):
    used, at, turn = [[], [], []], {}, 0
    for engines, s in steps:
        kind = s[0]
        if T not in engines:
            continue
        if kind in ("context", "bc", "step_low", "step") or (kind == "conv" and s[2] == 0):
            keys, bank = [s[:2] if kind == "conv" else s], 2
        elif kind == "project":
            keys, bank = [("project", i) for i in range(3)], 2
        elif kind in ("residual", "normed"):
            keys, bank = [s], 0
        elif kind in ("gate", "up", "wins"):
            keys, bank = [s], None
        elif kind == "taps":
            keys, bank = [("taps", i) for i in range(2)], None
        elif kind == "down" and s[2] % 3 == 0:
            keys, bank = [("down", s[1], s[2] // 3)], 1 + s[2] // 3
        else:
            continue
        for key in keys:
            n = bank
            if n is None:
                n, turn = turn, 1 - turn
            at[key] = (n, len(used[n]), used[n][-1] if used[n] else None)
            used[n].append(key)
    return at


def group(k, half):
    within = k % (UNITS // C)
    quad = 2 * (within % 2) + half
    return quad * SETS + within // 2, quad


def gated_block(nc, x, ctx_in, g_mix, g_ffn, in_w, conv_w, conv_b, xproj_w, step_w, step_b, a_log, skip,
                w_gate, w_up, w_down, out):
    F32, BF16, F32R = mybir.dt.float32, mybir.dt.bfloat16, mybir.dt.float32r
    ALU, ACT = mybir.AluOpType, mybir.ActivationFunctionType
    STEPS = order()
    BANK = banks(STEPS)

    with ExitStack() as stack:
        def sb(name, shape, dt=F32):
            return stack.enter_context(nc.sbuf_tensor(name, shape, dt))

        def sem(name):
            return stack.enter_context(nc.semaphore(name))

        x_sb = sb("x_sb", [P, B, C, L])
        ctx_sb = sb("ctx_sb", [P, B, C, D_CTX])
        in_w_sb = sb("in_w_sb", [P, C, D_CTX])
        conv_w_sb = sb("conv_w_sb", [P, C, TAPS])
        conv_b_sb = sb("conv_b_sb", [P, C])
        step_b_sb = sb("step_b_sb", [P, C])
        skip_sb = sb("skip_sb", [P, C])
        xproj_sb = sb("xproj_sb", [DR + 2 * NS, D_IN])
        step_w_sb = sb("step_w_sb", [P, C, DR])
        a_log_sb = sb("a_log_sb", [GROUPS, P])
        gains_sb = sb("gains_sb", [P, 2])
        up_raw = sb("up_raw", [P, KB, 2, HID])
        down_sb = sb("down_sb", [P, IC, 4, D_IN])
        ident = sb("ident", [P, P])
        plus_b = sb("plus_b", [P, P], BF16)
        minus_b = sb("minus_b", [P, P], BF16)
        spread_f = sb("spread_f", [P, ES, P])
        spread_r = sb("spread_r", [P, ES, P], F32R)
        gather = sb("gather", [P, SETS, 32])
        power = sb("power", [P, C])
        taps_d = sb("taps_d", [P, C, TAPS, P])
        in_taps = sb("in_taps", [P, TAPS, D_IN])
        xproj_t = sb("xproj_t", [P, C, DR + 2 * NS])
        b_wide = sb("b_wide", [P, C, P])
        c_wide = sb("c_wide", [P, C, P])
        step_wt = sb("step_wt", [DR, D_IN])
        a_exp = sb("a_exp", [P, GROUPS])
        a_neg = sb("a_neg", [P, GROUPS])
        gains = sb("gains", [P, 2])
        up_hi = sb("up_hi", [P, KB, 2, 4, D_IN], F32R)
        up_lo = sb("up_lo", [P, KB, 2, 4, D_IN], F32R)
        ctx_t = sb("ctx_t", [P, 2, TAPS - 1 + L])
        stats = sb("stats", [P, B, C, 6])
        moments = sb("moments", [P, B, C, 2])
        veps = sb("veps", [P, B, C])
        rstd = sb("rstd", [P, B, C])
        shift = sb("shift", [P, B, C])
        z_gate = sb("z_gate", [P, 2, C, L])
        u = sb("u", [P, 2, C, L])
        bc = sb("bc", [P, 2, 2, L])
        low = sb("low", [DR, 2, L])
        sp_abs = sb("sp_abs", [P, C, L])
        sp_exp = sb("sp_exp", [P, C, L])
        sp_pos = sb("sp_pos", [P, C, L])
        sp_ln = sb("sp_ln", [P, C, L])
        sp_back = sb("sp_back", [P, C, L])
        sp_lost = sb("sp_lost", [P, C, L])
        delta = sb("delta", [P, C, L])
        du = sb("du", [P, C, L])
        delta_h = sb("delta_h", [P, 2, 2, C, L], F32R)
        du_h = sb("du_h", [P, 2, 2, C, L], F32R)
        decay = sb("decay", [P, N_DECAY, 2, L])
        state = sb("state", [P, N_STATE, 2, L])
        prod = sb("prod", [P, N_PROD, 2, L])
        mixed = sb("mixed", [P, C, L])
        x2 = x_sb
        stats2 = sb("stats2", [P, B, C, 6])
        moments2 = sb("moments2", [P, B, C, 2])
        veps2 = sb("veps2", [P, B, C])
        rstd2 = sb("rstd2", [P, B, C])
        xn = sb("xn", [P, C, L])
        xnt_hi = sb("xnt_hi", [P, KB, L], F32R)
        xnt_lo = sb("xnt_lo", [P, KB, L], F32R)
        gate_s = up_raw[:, 0].rearrange("p w (j t) -> p w j t", j=4)
        h = sb("h", [P, IC, 4, L])
        h_abs = up_raw[:, 1].rearrange("p w (j t) -> p w j t", j=4)
        beats = sb("beats", [P, IC, 6, L], BF16)
        h_kept = sb("h_kept", [P, IC, 4, L])
        result = sb("result", [P, 2, C, L])

        dec_ps = [stack.enter_context(nc.psum_tensor(f"dec_ps{i}", [P, 2, L], F32)) for i in range(2)]
        drv_ps = [stack.enter_context(nc.psum_tensor(f"drv_ps{i}", [P, 2, L], F32)) for i in range(2)]
        y_ps = stack.enter_context(nc.psum_tensor("y_ps", [P, C, L], F32))
        work = [stack.enter_context(nc.psum_tensor(f"work{i}", [P, 2, L], F32)) for i in range(3)]

        ctx_loaded = [sem(f"ctx_loaded{b}") for b in range(B)]
        x_loaded = [sem(f"x_loaded{b}") for b in range(B)]
        taps_loaded, small_loaded = sem("taps_loaded"), sem("small_loaded")
        up_loaded, down_loaded = sem("up_loaded"), sem("down_loaded")
        stored = [sem(f"stored{i}") for i in range(4)]
        blank, masks_ready, pads_ready = sem("blank"), sem("masks_ready"), sem("pads_ready")
        masks_cast, diags_ready, taps_ready = sem("masks_cast"), sem("diags_ready"), sem("taps_ready")
        project_ready, a_raw, a_ready, gains_ready = sem("project_ready"), sem("a_raw"), sem("a_ready"), sem("gains_ready")
        hi_ready, lo_ready = sem("hi_ready"), sem("lo_ready")
        filled = [sem(f"filled{i}") for i in range(3)]
        ctx_turned = sem("ctx_turned")
        x_stats, x_moments, x_veps, x_rstd, x_shift = (sem(n) for n in ("x_stats", "x_moments", "x_veps", "x_rstd", "x_shift"))
        u_ready, z_ready, bc_ready, low_ready = (sem(n) for n in ("u_ready", "z_ready", "bc_ready", "low_ready"))
        abs_ready, pos_ready, exp_ready, ln_ready = (sem(n) for n in ("abs_ready", "pos_ready", "exp_ready", "ln_ready"))
        back_ready, lost_ready, sum_ready, delta_ready, du_ready = (
            sem(n) for n in ("back_ready", "lost_ready", "sum_ready", "delta_ready", "du_ready"))
        delta_hi, delta_lo, du_hi, du_lo = (sem(n) for n in ("delta_hi", "delta_lo", "du_hi", "du_lo"))
        zero_col = sem("zero_col")
        delta_spread, du_spread, decay_ready, drive_ready, scanned, prod_ready, summed = (
            sem(n) for n in ("delta_spread", "du_spread", "decay_ready", "drive_ready", "scanned", "prod_ready", "summed"))
        skip_added, mixed_ready, x2_ready = sem("skip_added"), sem("mixed_ready"), sem("x2_ready")
        s_stats, s_moments, s_veps, s_rstd, xn_ready = (sem(n) for n in ("s_stats", "s_moments", "s_veps", "s_rstd", "xn_ready"))
        xnt_hi_ready, xnt_lo_ready, gate_ready, h_ready, h_abs_ready = (
            sem(n) for n in ("xnt_hi_ready", "xnt_lo_ready", "gate_ready", "h_ready", "h_abs_ready"))
        beats_ready, kept_ready, result_ready = (
            sem(n) for n in ("beats_ready", "kept_ready", "result_ready"))

        block = stack.enter_context(nc.Block())

        def steps_of(engine):
            return [step for engines, step in STEPS if engine in engines]

        def has(eng, key):
            n, before, _ = BANK[key]
            eng.wait_ge(filled[n], before + 1)
            return work[n]

        def last_read(key):
            kind, b = key[0], key[1]
            if kind == "wins":
                return kept_ready, 8 * b + 4 * key[2] + 2 * key[3] + 2
            return {
                "taps": lambda: (taps_ready, b + 1), "project": lambda: (project_ready, b + 1),
                "context": lambda: (ctx_turned, b + 1), "conv": lambda: (u_ready, b + 1),
                "bc": lambda: (bc_ready, b + 1), "step_low": lambda: (low_ready, b + 1),
                "step": lambda: (pos_ready, b + 1), "residual": lambda: (x2_ready, C * (b + 1)),
                "normed": lambda: (xnt_lo_ready, b + 1), "gate": lambda: (gate_ready, 4 * b + key[2] + 1),
                "up": lambda: (h_ready, 4 * b + key[2] + 1), "down": lambda: (result_ready, 2 * b + key[2] + 1),
            }[kind]()

        def index(b, k):
            return UNITS * b + k

        @block.sync
        def _(sp):
            sp.dma_start(in_w_sb[:], in_w.rearrange("(c p) d -> p c d", p=P)).then_inc(taps_loaded, 16)
            sp.dma_start(conv_w_sb[:], conv_w.rearrange("(c p) k -> p c k", p=P)).then_inc(taps_loaded, 16)
            sp.dma_start(ctx_sb[:, 0], ctx_in[0].rearrange("(c p) d -> p c d", p=P)).then_inc(ctx_loaded[0], 16)
            sp.dma_start(x_sb[:, 0], x[0].rearrange("(c p) d -> p c d", p=P)).then_inc(x_loaded[0], 16)
            for dst, src in ((conv_b_sb, conv_b), (step_b_sb, step_b), (skip_sb, skip)):
                sp.dma_start(dst[:], src.rearrange("(c p) -> p c", p=P), allow_slow_non_contiguous=True).then_inc(small_loaded, 16)
            sp.dma_start(xproj_sb[:], xproj_w).then_inc(small_loaded, 16)
            sp.dma_start(step_w_sb[:], step_w.rearrange("(c p) r -> p c r", p=P)).then_inc(small_loaded, 16)
            sp.dma_start(a_log_sb[:], a_log.rearrange("(g e) n -> g (e n)", e=ES)).then_inc(small_loaded, 16)
            sp.dma_start(gains_sb[:, 0:1], g_mix[None, :].broadcast_to([P, 1])).then_inc(small_loaded, 16)
            sp.dma_start(gains_sb[:, 1:2], g_ffn[None, :].broadcast_to([P, 1])).then_inc(small_loaded, 16)
            for b in range(1, B):
                sp.dma_start(ctx_sb[:, b], ctx_in[b].rearrange("(c p) d -> p c d", p=P)).then_inc(ctx_loaded[b], 16)
                sp.dma_start(x_sb[:, b], x[b].rearrange("(c p) d -> p c d", p=P)).then_inc(x_loaded[b], 16)
            sp.dma_start(up_raw[:, :, 0], w_gate.rearrange("(k p) i -> p k i", p=P)).then_inc(up_loaded, 16)
            sp.dma_start(up_raw[:, :, 1], w_up.rearrange("(k p) i -> p k i", p=P)).then_inc(up_loaded, 16)
            sp.dma_start(down_sb[:], w_down.rearrange("(c p j) n -> p c j n", p=P, j=4)).then_inc(down_loaded, 16)
            for b in range(B):
                for tt in range(2):
                    sp.wait_ge(result_ready, 2 * b + tt + 1)
                    sp.dma_start(out[b, tt * P:(tt + 1) * P], result[:, b % 2, tt]).then_inc(stored[2 * (b % 2) + tt], 16)
            for i in range(4):
                sp.wait_ge(stored[i], 16 * B // 2)

        @block.gpsimd
        def _(pool):
            for step in steps_of(G):
                kind, b = step[0], step[1] if len(step) > 1 else None
                if kind == "masks":
                    pool.memset(ident[:], 0.0).then_inc(blank, 1)
                    pool.memset(ctx_t[:, :, 0:TAPS - 1], 0.0).then_inc(pads_ready, 1)
                    pool.memset(spread_f[:], 0.0).then_inc(blank, 1)
                    pool.memset(gather[:], 1.0).then_inc(blank, 1)
                    pool.memset(power[:], -0.5).then_inc(pads_ready, 1)
                    pool.memset(decay[:, :, :, 0:1], 0.0).then_inc(zero_col, 1)
                    pool.wait_ge(blank, 3)
                    pool.affine_select(out=ident[:], in_=ident[:], compare_op=ALU.not_equal, fill=1.0, base=0,
                                       pattern=[[-1, P]], channel_multiplier=1).then_inc(masks_ready, 1)
                    wide = spread_f[:].rearrange("p g (e n) -> p g e n", n=NS)
                    for rows, base in ((0, 0), (1, -64)):
                        pool.affine_select(out=wide, in_=wide, compare_op=ALU.not_equal, fill=1.0, base=base,
                                           pattern=[[-ES, ES], [-1, ES], [0, NS]],
                                           channel_multiplier=1).then_inc(masks_ready, 1)
                        pool.wait_ge(masks_ready, 2 + rows)
                    pool.affine_select(out=gather[:], in_=gather[:], compare_op=ALU.is_ge, fill=0.0, base=0,
                                       pattern=[[P, SETS], [-NS, 32]], channel_multiplier=1).then_inc(masks_ready, 1)
                    pool.wait_ge(masks_ready, 4)
                    pool.affine_select(out=gather[:], in_=gather[:], compare_op=ALU.is_ge, fill=0.0, base=NS - 1,
                                       pattern=[[-P, SETS], [NS, 32]], channel_multiplier=-1).then_inc(masks_ready, 1)
                elif kind == "context":
                    pool.wait_ge(pads_ready, 2)
                    pool.wait_ge(x_veps, b + 1)
                    pool.tensor_tensor(rstd[:, b], veps[:, b], power[:], ALU.pow).then_inc(x_rstd, 1)
                elif kind == "split_up":
                    k, w = divmod(step[1], 2)
                    pool.wait_ge(hi_ready, step[1] + 1)
                    pool.tensor_tensor(up_lo[:, k, w], up_raw[:, k, w].rearrange("p (g j) -> p j g", j=4),
                                       up_hi[:, k, w].bitcast(F32), ALU.subtract).then_inc(lo_ready, 1)
                elif kind == "softplus":
                    pool.wait_ge(pos_ready, b + 1)
                    pool.wait_ge(ln_ready, b + 1)
                    if b:
                        pool.wait_ge(delta_ready, b)
                    pool.tensor_tensor(sp_abs[:], sp_pos[:], sp_ln[:], ALU.add).then_inc(sum_ready, 1)
                elif kind == "delta":
                    pool.wait_ge(delta_ready, b + 1)
                    if b:
                        pool.wait_ge(du_lo, 2 * b)
                    pool.tensor_tensor(du[:], delta[:], u[:, b % 2], ALU.mult).then_inc(du_ready, 1)
                elif kind == "unit":
                    n = index(*step[1:])
                    pool.wait_ge(scanned, n + 1)
                    pool.wait_ge(bc_ready, b + 1)
                    if n >= N_PROD:
                        pool.wait_ge(summed, (n - N_PROD) // 2 + 1)
                    pool.tensor_tensor(prod[:, n % N_PROD], state[:, n % N_STATE],
                                       bc[:, b % 2, 1:2].broadcast_to([P, 2, L]), ALU.mult).then_inc(prod_ready, 1)
                elif kind == "residual":
                    pool.wait_ge(s_veps, b + 1)
                    pool.tensor_tensor(rstd2[:, b], veps2[:, b], power[:], ALU.pow).then_inc(s_rstd, 1)

        @block.scalar
        def _(act):
            def decay_of(n):
                b, k = divmod(n, UNITS)
                act.wait_ge(delta_spread, n + 1)
                if n == 0:
                    act.wait_ge(zero_col, 1)
                if n >= N_DECAY:
                    act.wait_ge(scanned, n - N_DECAY + 1)
                for half in range(2):
                    g, _ = group(k, half)
                    col = (k // (UNITS // C)) * (GROUPS // C) + g
                    last = act.activation(decay[:, n % N_DECAY, half, 1:L], dec_ps[n % 2][:, half, 1:L], ACT.Exp,
                                          scale=a_neg[:, col:col + 1])
                last.then_inc(decay_ready, 1)

            for step in steps_of(A):
                kind, b = step[0], step[1] if len(step) > 1 else None
                if kind == "load":
                    act.preload_act_table_set("silu_and_others")
                elif kind == "masks":
                    act.wait_ge(small_loaded, 16 * 8)
                    act.activation(gains[:], gains_sb[:], ACT.Tanh).then_inc(gains_ready, 1)
                    act.wait_ge(masks_ready, 5)
                    act.activation(spread_r[:], spread_f[:], ACT.Copy).then_inc(masks_cast, 1)
                    act.activation(plus_b[:], ident[:], ACT.Copy).then_inc(masks_cast, 1)
                    act.activation(minus_b[:], ident[:], ACT.Copy, scale=-1.0).then_inc(masks_cast, 1)
                elif kind == "taps":
                    for i in range(2):
                        bank = has(act, ("taps", i))
                        act.activation(in_taps[:, 2 * i:2 * i + 2, :], bank[:], ACT.Copy).then_inc(taps_ready, 1)
                elif kind == "project":
                    act.wait_ge(project_ready, 2)
                    bank = has(act, ("project", 2))
                    act.activation(a_exp[:], bank[:, 0, 0:GROUPS], ACT.Copy).then_inc(project_ready, 1)
                elif kind == "context":
                    bank = has(act, step)
                    if b:
                        act.wait_ge(pads_ready, 1)
                    if b >= 2:
                        has(act, ("conv", b - 2))
                    act.activation(ctx_t[:, b % 2, TAPS - 1:], bank[:].rearrange("p a t -> p (a t)")[:, 0:L],
                                   ACT.Copy).then_inc(ctx_turned, 1)
                elif kind == "gate_in":
                    act.preload_act_table_set("silu_and_others")
                    bank = has(act, ("conv", b))
                    if b >= 2:
                        act.wait_ge(mixed_ready, C * (b - 1))
                    for c in range(C):
                        last = act.activation(u[:, b % 2, c], bank[:, c], ACT.Silu, bias=conv_b_sb[:, c:c + 1])
                    last.then_inc(u_ready, 1)
                    act.wait_ge(x_shift, b + 1)
                    for c in range(C):
                        last = act.activation(z_gate[:, b % 2, c], x_sb[:, b, c], ACT.Silu, bias=shift[:, b, c:c + 1],
                                              scale=rstd[:, b, c:c + 1])
                    last.then_inc(z_ready, 1)
                    act.preload_act_table_set("natural_log_exp_and_others")
                elif kind == "bc":
                    bank = has(act, step)
                    if b >= 2:
                        act.wait_ge(prod_ready, UNITS * (b - 1))
                    act.activation(bc[:, b % 2], bank[:], ACT.Copy).then_inc(bc_ready, 1)
                elif kind == "step_low":
                    bank = has(act, step)
                    act.activation(low[:, b % 2], bank[0:DR, 0], ACT.Copy).then_inc(low_ready, 1)
                elif kind == "softplus":
                    bank = has(act, ("step", b))
                    if b:
                        act.wait_ge(exp_ready, b)
                        act.wait_ge(sum_ready, b)
                        act.wait_ge(delta_ready, b)
                    for c in range(C):
                        last = act.activation(sp_abs[:, c], bank[:, c], ACT.Abs, bias=step_b_sb[:, c:c + 1])
                    last.then_inc(abs_ready, 1)
                    for c in range(C):
                        last = act.activation(sp_pos[:, c], bank[:, c], ACT.Relu, bias=step_b_sb[:, c:c + 1])
                    last.then_inc(pos_ready, 1)
                    act.wait_ge(abs_ready, b + 1)
                    act.activation(sp_exp[:], sp_abs[:], ACT.Exp, scale=-1.0).then_inc(exp_ready, 1)
                    act.wait_ge(exp_ready, b + 1)
                    act.activation(sp_ln[:], sp_exp[:], ACT.Ln, bias=1.0).then_inc(ln_ready, 1)
                elif kind == "halves":
                    if b >= 2:
                        act.wait_ge(du_spread, UNITS * (b - 1))
                        act.wait_ge(delta_spread, UNITS * (b - 1))
                    src, dst, ready, done = ((delta, delta_h, delta_ready, delta_hi), (du, du_h, du_ready, du_hi))[step[2]]
                    act.wait_ge(ready, b + 1)
                    for q in range(2):
                        rows = slice(64 * q, 64 * q + 64)
                        act.activation(dst[rows, b % 2, q], src[rows], ACT.Copy).then_inc(done, 1)
                elif kind == "tables":
                    act.wait_ge(project_ready, 3)
                    act.activation(a_neg[:], a_exp[:], ACT.Exp).then_inc(a_raw, 1)
                    act.wait_ge(a_raw, 1)
                    act.activation(a_exp[:], a_neg[:], ACT.Copy, scale=-1.0).then_inc(a_raw, 1)
                    act.wait_ge(a_raw, 2)
                    act.activation(a_neg[:], a_exp[:], ACT.Copy).then_inc(a_ready, 1)
                    act.wait_ge(a_ready, 1)
                elif kind == "ahead":
                    for n in range(SPREAD_AHEAD - 1):
                        decay_of(n)
                elif kind == "unit":
                    n = index(*step[1:]) + SPREAD_AHEAD - 1
                    if n < UNITS * B:
                        decay_of(n)
                elif kind == "split_up":
                    k, w = divmod(step[1], 2)
                    act.wait_ge(up_loaded, 32)
                    act.activation(up_hi[:, k, w], up_raw[:, k, w].rearrange("p (g j) -> p j g", j=4),
                                   ACT.Copy).then_inc(hi_ready, 1)
                elif kind == "normed":
                    bank = has(act, step)
                    if b:
                        has(act, ("up", b - 1, 3))
                    act.activation(xnt_hi[:], bank[:], ACT.Copy).then_inc(xnt_hi_ready, 1)
                elif kind == "gate":
                    i = step[2]
                    if i == 0:
                        act.preload_act_table_set("silu_and_others")
                    bank = has(act, step)
                    if b:
                        act.wait_ge(h_ready, 4 * (b - 1) + i + 1)
                    act.activation(gate_s[:, i // 2, 2 * (i % 2):2 * (i % 2) + 2], bank[:],
                                   ACT.Silu).then_inc(gate_ready, 1)
                    if i == 3 and b < B - 1:
                        act.preload_act_table_set("natural_log_exp_and_others")
                elif kind == "compare":
                    c = step[2]
                    act.wait_ge(h_ready, 4 * b + 2 * c + 2)
                    if b:
                        act.wait_ge(beats_ready, 3 * (2 * (b - 1) + c + 1))
                    act.activation(h_abs[:, c], h[:, c], ACT.Abs).then_inc(h_abs_ready, 1)

        @block.vector
        def _(dve):
            for step in steps_of(V):
                kind, b = step[0], step[1] if len(step) > 1 else None
                if kind == "taps":
                    dve.wait_ge(taps_loaded, 32)
                    dve.wait_ge(masks_ready, 1)
                    for c in range(C):
                        for k in range(TAPS):
                            last = dve.tensor_scalar(taps_d[:, c, k], ident[:], conv_w_sb[:, c, k:k + 1], None, ALU.mult)
                        last.then_inc(diags_ready, 1)
                elif kind == "project":
                    bank = has(dve, ("project", 0))
                    W = DR + 2 * NS
                    src = bank[:, :, 0:W]
                    dve.tensor_copy(xproj_t[:], src)
                    dve.tensor_copy(b_wide[:].rearrange("p c (e n) -> p c e n", n=NS),
                                    src[:, :, None, DR:DR + NS].broadcast_to([P, C, ES, NS]))
                    dve.tensor_copy(c_wide[:].rearrange("p c (e n) -> p c e n", n=NS),
                                    src[:, :, None, DR + NS:W].broadcast_to([P, C, ES, NS])).then_inc(project_ready, 1)
                    bank = has(dve, ("project", 1))
                    dve.tensor_copy(step_wt[:], bank[0:DR].rearrange("p a t -> p (a t)")[:, 0:D_IN]).then_inc(project_ready, 1)
                elif kind == "context":
                    dve.wait_ge(x_loaded[b], 16)
                    for c in range(C):
                        dve.bn_stats(stats[:, b, c], x_sb[:, b, c]).then_inc(x_stats, 1)
                    for c in range(C):
                        dve.wait_ge(x_stats, C * b + c + 1)
                        dve.bn_aggr(moments[:, b, c], stats[:, b, c]).then_inc(x_moments, 1)
                    dve.wait_ge(x_moments, C * (b + 1))
                    dve.tensor_scalar(veps[:, b], moments[:, b, :, 1], EPS, None, ALU.add).then_inc(x_veps, 1)
                    dve.wait_ge(x_rstd, b + 1)
                    dve.scalar_tensor_tensor(shift[:, b], moments[:, b, :, 0], -1.0, rstd[:, b], ALU.mult,
                                             ALU.mult).then_inc(x_shift, 1)
                elif kind == "softplus":
                    dve.wait_ge(exp_ready, b + 1)
                    dve.tensor_scalar(sp_back[:], sp_exp[:], 1.0, 1.0, ALU.add, ALU.subtract).then_inc(back_ready, 1)
                    dve.wait_ge(back_ready, b + 1)
                    dve.tensor_tensor(sp_lost[:], sp_exp[:], sp_back[:], ALU.subtract).then_inc(lost_ready, 1)
                elif kind == "delta":
                    dve.wait_ge(lost_ready, b + 1)
                    dve.wait_ge(sum_ready, b + 1)
                    if b:
                        dve.wait_ge(delta_lo, 2 * b)
                        dve.wait_ge(delta_hi, 2 * b)
                        dve.wait_ge(du_ready, b)
                    dve.tensor_tensor(delta[:], sp_abs[:], sp_lost[:], ALU.add).then_inc(delta_ready, 1)
                elif kind == "halves":
                    src, dst, hi, done = ((delta, delta_h, delta_hi, delta_lo), (du, du_h, du_hi, du_lo))[step[2]]
                    for q in range(2):
                        dve.wait_ge(hi, 2 * b + q + 1)
                        rows, other = slice(64 * q, 64 * q + 64), slice(64 - 64 * q, 128 - 64 * q)
                        dve.tensor_tensor(dst[other, b % 2, q], src[rows], dst[rows, b % 2, q].bitcast(F32),
                                          ALU.subtract).then_inc(done, 1)
                elif kind == "unit":
                    n = index(*step[1:])
                    dve.wait_ge(du_spread, n + 1)
                    dve.wait_ge(bc_ready, b + 1)
                    drive = drv_ps[n % 2]
                    dve.tensor_tensor(drive[:], drive[:], bc[:, b % 2, 0:1].broadcast_to([P, 2, L]),
                                      ALU.mult).then_inc(drive_ready, 1)
                    dve.wait_ge(drive_ready, n + 1)
                    dve.wait_ge(decay_ready, n + 1)
                    if n >= N_STATE:
                        dve.wait_ge(prod_ready, n - N_STATE + 1)
                    dve.tensor_tensor_scan(state[:, n % N_STATE].rearrange("p a t -> p (a t)"),
                                           decay[:, n % N_DECAY].rearrange("p a t -> p (a t)"),
                                           drive[:].rearrange("p a t -> p (a t)"), 0.0, ALU.mult,
                                           ALU.add).then_inc(scanned, 1)
                elif kind == "finish":
                    c = step[2]
                    n = C * b + c
                    dve.wait_ge(summed, UNITS // 2 // C * (n + 1))
                    dve.wait_ge(z_ready, b + 1)
                    dve.wait_ge(u_ready, b + 1)
                    if b:
                        has(dve, ("residual", b - 1))
                    dve.scalar_tensor_tensor(mixed[:, c], u[:, b % 2, c], skip_sb[:, c:c + 1], y_ps[:, c], ALU.mult,
                                             ALU.add).then_inc(skip_added, 1)
                    dve.wait_ge(skip_added, n + 1)
                    dve.tensor_tensor(mixed[:, c], mixed[:, c], z_gate[:, b % 2, c], ALU.mult).then_inc(mixed_ready, 1)
                elif kind == "residual":
                    bank = has(dve, step)
                    dve.wait_ge(gains_ready, 1)
                    dve.wait_ge(x_loaded[b], 16)
                    for c in range(C):
                        last = dve.scalar_tensor_tensor(x2[:, b, c], bank[:, c], gains[:, 0:1], x_sb[:, b, c],
                                                        ALU.mult, ALU.add)
                        last.then_inc(x2_ready, 1)
                    dve.wait_ge(x2_ready, C * (b + 1))
                    for c in range(C):
                        dve.bn_stats(stats2[:, b, c], x2[:, b, c]).then_inc(s_stats, 1)
                    for c in range(C):
                        dve.wait_ge(s_stats, C * b + c + 1)
                        dve.bn_aggr(moments2[:, b, c], stats2[:, b, c]).then_inc(s_moments, 1)
                    dve.wait_ge(s_moments, C * (b + 1))
                    dve.tensor_scalar(veps2[:, b], moments2[:, b, :, 1], EPS, None, ALU.add).then_inc(s_veps, 1)
                elif kind == "norm":
                    dve.wait_ge(s_rstd, b + 1)
                    if b:
                        has(dve, ("normed", b - 1))
                    for c in range(C):
                        dve.tensor_scalar(xn[:, c], x2[:, b, c], moments2[:, b, c, 0:1], rstd2[:, b, c:c + 1],
                                          ALU.subtract, ALU.mult).then_inc(xn_ready, 1)
                elif kind == "normed":
                    bank = has(dve, step)
                    dve.wait_ge(xnt_hi_ready, b + 1)
                    dve.tensor_tensor(xnt_lo[:], bank[:], xnt_hi[:].bitcast(F32), ALU.subtract).then_inc(xnt_lo_ready, 1)
                elif kind == "up":
                    i = step[2]
                    bank = has(dve, step)
                    dve.wait_ge(gate_ready, 4 * b + i + 1)
                    if b:
                        dve.wait_ge(kept_ready, 8 * (b - 1) + 4 * (i // 2) + 4)
                        dve.wait_ge(h_abs_ready, 2 * (b - 1) + i // 2 + 1)
                    mem = slice(2 * (i % 2), 2 * (i % 2) + 2)
                    dve.tensor_tensor(h[:, i // 2, mem], gate_s[:, i // 2, mem], bank[:], ALU.mult).then_inc(h_ready, 1)
                elif kind == "compare":
                    c = step[2]
                    n = 2 * b + c
                    dve.wait_ge(h_abs_ready, n + 1)
                    if b:
                        has(dve, ("wins", b - 1, c, 1))
                    for at, m, d in ((0, 3, 1), (3, 2, 2), (5, 1, 3)):
                        dve.tensor_tensor(beats[:, c, at:at + m], h_abs[:, c, 0:m], h_abs[:, c, d:d + m],
                                          ALU.is_ge).then_inc(beats_ready, 1)
                elif kind == "wins":
                    _, _, c, pair = step
                    bank = has(dve, step)
                    dve.wait_ge(h_ready, 4 * b + 2 * c + 2)
                    if b:
                        has(dve, ("down", b - 1, 1))
                    for m in range(2):
                        j = 2 * pair + m
                        last = dve.scalar_tensor_tensor(h_kept[:, c, j], bank[:, m], 1.5 - j, h[:, c, j],
                                                        ALU.is_ge, ALU.mult)
                        last.then_inc(kept_ready, 1)
                elif kind == "down" and step[2] % 3 == 2:
                    tt = step[2] // 3
                    key = ("down", b, tt)
                    bank = has(dve, key)
                    if b >= 2:
                        dve.wait_ge(stored[2 * (b % 2) + tt], 16 * (b // 2))
                    dve.scalar_tensor_tensor(result[:, b % 2, tt], bank[:, 0], gains[:, 1:2],
                                             x2[:, b, tt], ALU.mult, ALU.add).then_inc(result_ready, 1)

        @block.tensor
        def _(pe):
            def take(key):
                n, _, prior = BANK[key]
                if prior:
                    pe.wait_ge(*last_read(prior))
                return work[n]

            def spread(n, src, dst, ready):
                b, k = divmod(n, UNITS)
                c = k // (UNITS // C)
                for half in range(2):
                    g, quad = group(k, half)
                    last = pe.matmul(dst[n % 2][:, half], spread_r[:, g % ES], src[:, b % 2, quad // 2, c],
                                     start=True, stop=True)
                last.then_inc(ready, 1)

            def spread_delta(n):
                if n % UNITS == 0:
                    pe.wait_ge(delta_hi, 2 * (n // UNITS + 1))
                    pe.wait_ge(delta_lo, 2 * (n // UNITS + 1))
                if n >= 2:
                    pe.wait_ge(decay_ready, n - 1)
                spread(n, delta_h, dec_ps, delta_spread)

            def spread_du(n):
                if n % UNITS == 0:
                    pe.wait_ge(du_hi, 2 * (n // UNITS + 1))
                    pe.wait_ge(du_lo, 2 * (n // UNITS + 1))
                if n >= 2:
                    pe.wait_ge(scanned, n - 1)
                spread(n, du_h, drv_ps, du_spread)

            def sum_states(s):
                b, r = divmod(s, UNITS // 2)
                c, r = divmod(r, SETS)
                pe.wait_ge(prod_ready, 2 * s + 2)
                if r == 0 and s >= SETS:
                    pe.wait_ge(skip_added, C * b + c)
                for quad in range(QUADS):
                    n = 2 * s + quad // 2
                    last = pe.matmul(y_ps[32 * quad:32 * quad + 32, c], gather[:, r], prod[:, n % N_PROD, quad % 2],
                                     start=(r == 0), stop=(r == SETS - 1), tile_position=(0, 32 * quad))
                last.then_inc(summed, 1)

            for step in steps_of(T):
                kind, b = step[0], step[1] if len(step) > 1 else None
                if kind == "taps":
                    for i in range(2):
                        bank = take(("taps", i))
                        for k in range(2):
                            for c in range(C):
                                pe.wait_ge(diags_ready, c + 1)
                                last = pe.matmul(bank[:, k, c * P:(c + 1) * P], in_w_sb[:, c], taps_d[:, c, 2 * i + k],
                                                 start=True, stop=True)
                        last.then_inc(filled[BANK["taps", i][0]], 1)
                elif kind == "project":
                    pe.wait_ge(small_loaded, 16 * 8)
                    bank = take(("project", 0))
                    W = DR + 2 * NS
                    for c in range(C):
                        last = pe.transpose(bank[:, c, 0:W], xproj_sb[:, c * P:(c + 1) * P], ident[0:W, 0:W])
                    last.then_inc(filled[2], 1)
                    bank = take(("project", 1))
                    for c in range(C):
                        last = pe.transpose(bank[0:DR, 0, c * P:(c + 1) * P], step_w_sb[:, c], ident[:])
                    last.then_inc(filled[2], 1)
                    bank = take(("project", 2))
                    pe.transpose(bank[:, 0, 0:GROUPS], a_log_sb[:], ident[0:GROUPS, 0:GROUPS]).then_inc(filled[2], 1)
                elif kind == "context":
                    pe.wait_ge(ctx_loaded[b], 16)
                    bank = take(step)
                    for c in range(C):
                        last = pe.transpose(bank[:, 0, c * P:(c + 1) * P], ctx_sb[:, b, c], ident[:])
                    last.then_inc(filled[2], 1)
                elif kind == "conv":
                    q = step[2]
                    c = q // 2
                    if q == 0:
                        take(("conv", b))
                        pe.wait_ge(ctx_turned, b + 1)
                        pe.wait_ge(pads_ready, 1)
                        if b == 0:
                            pe.wait_ge(taps_ready, 2)
                    bank = work[BANK["conv", b][0]]
                    for k in range(2 * (q % 2), 2 * (q % 2) + 2):
                        last = pe.matmul(bank[:, c], in_taps[:, k, c * P:(c + 1) * P], ctx_t[:, b % 2, k:k + L],
                                         start=(k == 0), stop=(k == TAPS - 1))
                    if q == 3:
                        last.then_inc(filled[BANK["conv", b][0]], 1)
                elif kind == "bc":
                    pe.wait_ge(u_ready, b + 1)
                    bank = take(step)
                    if b == 0:
                        pe.wait_ge(project_ready, 2)
                    for i, w in enumerate((b_wide, c_wide)):
                        for c in range(C):
                            last = pe.matmul(bank[:, i], w[:, c], u[:, b % 2, c], start=(c == 0), stop=(c == C - 1))
                    last.then_inc(filled[2], 1)
                elif kind == "step_low":
                    bank = take(step)
                    for c in range(C):
                        last = pe.matmul(bank[0:DR, 0], xproj_t[:, c, 0:DR], u[:, b % 2, c], start=(c == 0), stop=(c == C - 1))
                    last.then_inc(filled[2], 1)
                elif kind == "step":
                    pe.wait_ge(low_ready, b + 1)
                    bank = take(step)
                    for c in range(C):
                        last = pe.matmul(bank[:, c], step_wt[:, c * P:(c + 1) * P], low[:, b % 2], start=True, stop=True)
                    last.then_inc(filled[2], 1)
                elif kind == "ahead":
                    pe.wait_ge(masks_cast, 3)
                    for n in range(SPREAD_AHEAD):
                        spread_delta(n)
                    spread_du(0)
                elif kind == "unit":
                    n = index(*step[1:])
                    if n + 1 < UNITS * B:
                        spread_du(n + 1)
                    if n + SPREAD_AHEAD < UNITS * B:
                        spread_delta(n + SPREAD_AHEAD)
                    if n % 2 == 0 and n >= 4:
                        sum_states(n // 2 - 2)
                elif kind == "flush":
                    for s in range(UNITS * B // 2 - 2, UNITS * B // 2):
                        sum_states(s)
                elif kind == "residual":
                    pe.wait_ge(mixed_ready, C * (b + 1))
                    bank = take(step)
                    for lt in range(C):
                        for c in range(C):
                            last = pe.transpose(bank[:, lt, c * P:(c + 1) * P], mixed[:, c, lt * P:(lt + 1) * P], ident[:])
                    last.then_inc(filled[BANK[step][0]], 1)
                elif kind == "normed":
                    pe.wait_ge(xn_ready, C * (b + 1))
                    bank = take(step)
                    for k in range(KB):
                        for lt in range(C):
                            last = pe.transpose(bank[:, k, lt * P:(lt + 1) * P], xn[:, lt, k * P:(k + 1) * P], ident[:])
                    last.then_inc(filled[BANK[step][0]], 1)
                elif kind in ("gate", "up"):
                    i, w = step[2], 0 if kind == "gate" else 1
                    if i == 0 and w == 0:
                        pe.wait_ge(xnt_hi_ready, b + 1)
                        pe.wait_ge(xnt_lo_ready, b + 1)
                        if b == 0:
                            pe.wait_ge(hi_ready, 4)
                            pe.wait_ge(lo_ready, 4)
                    bank = take(step)
                    for m in range(2):
                        j = 2 * (i % 2) + m
                        cols = slice((i // 2) * P, (i // 2 + 1) * P)
                        terms = [(a, x_, k) for k in range(KB) for a, x_ in ((up_hi, xnt_lo), (up_lo, xnt_hi), (up_hi, xnt_hi))]
                        for t, (a, x_, k) in enumerate(terms):
                            last = pe.matmul(bank[:, m], a[:, k, w, j, cols], x_[:, k], start=(t == 0),
                                             stop=(t == len(terms) - 1))
                    last.then_inc(filled[BANK[step][0]], 1)
                elif kind == "wins":
                    _, _, c, pair = step
                    pe.wait_ge(beats_ready, 3 * (2 * b + c + 1))
                    bank = take(step)
                    terms = (((plus_b, 0), (plus_b, 3), (plus_b, 5)), ((minus_b, 0), (plus_b, 1), (plus_b, 4)),
                             ((minus_b, 3), (minus_b, 1), (plus_b, 2)), ((minus_b, 5), (minus_b, 4), (minus_b, 2)))
                    for m in range(2):
                        for t, (sign, at) in enumerate(terms[2 * pair + m]):
                            last = pe.matmul(bank[:, m], sign[:], beats[:, c, at], start=(t == 0), stop=(t == 2))
                    last.then_inc(filled[BANK[step][0]], 1)
                elif kind == "down":
                    q = step[2]
                    tt, third = divmod(q, 3)
                    key = ("down", b, tt)
                    if third == 0:
                        bank = take(key)
                        if b == 0:
                            pe.wait_ge(down_loaded, 16)
                        if q == 0:
                            pe.wait_ge(kept_ready, 8 * (b + 1))
                    bank = work[BANK[key][0]]
                    for n in range((0, 3, 6)[third], (3, 6, 8)[third]):
                        c, j = divmod(n, 4)
                        last = pe.matmul(bank[:, 0], h_kept[:, c, j, tt * P:(tt + 1) * P], down_sb[:, c, j],
                                         start=(n == 0), stop=(n == 7))
                    if third == 2:
                        last.then_inc(filled[BANK[key][0]], 1)


_INS = ['x', 'ctx_1024', 'g_xattn', 'g_ffn', 'L0_xattn_in_proj_w', 'L0_xattn_conv_w', 'L0_xattn_conv_b',
        'L0_xattn_x_proj_w', 'L0_xattn_dt_proj_w', 'L0_xattn_dt_proj_b', 'L0_xattn_A_log', 'L0_xattn_D',
        'L0_ffn_w_gate', 'L0_ffn_w_up', 'L0_ffn_w_down']


def kernel(**inputs):
    import numpy as _np
    import concourse.bacc as _bacc
    from concourse.bass_utils import run_bass_kernel_spmd as _run

    nc = _bacc.Bacc("TRN2", target_bir_lowering=False, num_devices=1)
    arrays, args = {}, []
    for name in _INS:
        a = _np.ascontiguousarray(inputs[name])
        arrays[f"in_{name}_dram"] = a
        args.append(nc.dram_tensor(f"in_{name}_dram", a.shape, mybir.dt.from_np(a.dtype), kind="ExternalInput").ap())
    args.append(nc.dram_tensor("out_dram", (B, L, D_IN), mybir.dt.float32, kind="ExternalOutput").ap())
    gated_block(nc, *args)
    r = _run(nc, [arrays], core_ids=[0])
    return r.results[0]["out_dram"]
```

```python
from contextlib import ExitStack

import concourse.bass as bass
from concourse import mybir

B, L, D_CTX, D_IN, NS, DR, TAPS, HID = 4, 256, 128, 256, 16, 8, 4, 1024
P = 128
C = D_IN // P
ES = P // NS
GROUPS = D_IN // ES
UNITS = GROUPS // 2
QUADS = 4
SETS = GROUPS // C // QUADS
KB = D_IN // P
IC = HID // (4 * P)
EPS = 1e-5

N_DECAY = 6
N_STATE = 4
N_PROD = 6
WORK = 3
WARM = 28
SPREAD_AHEAD = 4


T, A, V, G, S = "tensor", "scalar", "vector", "gpsimd", "sync"
ALL = (T, A, V, G, S)


FRONT = ("context", "shift", "conv", "gate_in", "x_dbl", "step", "bc", "softplus", "delta", "halves")


def order():
    steps = [((T, A), ("load",)), ((G,), ("masks",)), ((T, A), ("context", 0)), (ALL, ("taps",)), ((A,), ("masks",))]
    steps += [((T,), ("conv", 0, q)) for q in range(4)]
    steps += [((T, V), ("project",)), ((A,), ("gate_in", 0)), ((T, V), ("x_dbl", 0)), ((T, A), ("step", 0)),
              (ALL, ("softplus", 0)), ((A,), ("project",)), ((A,), ("tables",)), ((T, A), ("bc", 0)),
              (ALL, ("delta", 0)), ((A, V), ("halves", 0, 0)), ((A, V), ("halves", 0, 1)), (ALL, ("ahead",))]
    front = {n: [] for n in range(B * UNITS)}
    behind = {n: [] for n in range(B * UNITS)}

    def put(n, engines, *step):
        (front if step[0] in FRONT else behind)[n].append((engines, step))

    for b in range(B):
        first = UNITS * b

        n = first - UNITS
        if b >= 1:
            start = n - 3 if b >= 2 else n + 1
            if b >= 2:
                put(n - 5, (T, A), "context", b)
            for q in range(4):
                put(start + q, (T,), "conv", b, q)
            put(n + (1 if b >= 2 else 4), (A,), "gate_in", b)
            late = b == 1
            put(n + 5 + late, (T, V), "x_dbl", b)
            put(n + 6 + late, (T,), "step", b)
            put(n + 6 + late, (A,), "softplus", b)
            put(n + 7 + late, (V, G), "softplus", b)
            put(n + 7 + late, (G,), "delta", b)
            put(n + 10, (A, V), "halves", b, 0)
            put(n + 10, (T,), "bc", b)
            put(n + 11, (A, V, S), "halves", b, 1)
            put(n + 11, (A,), "bc", b)
        at = (4, 5, 12, 28)[b]
        put(at, (V, G), "context", b)
        put(at + 1, (V,), "shift", b)
        if b == 0:
            put(0, (T, A), "context", 1)
            put(12, (A,), "silu", -1)
            for i in range(4):
                put((1, 3, 13, 14)[i], (A, V, G), "split_up", i)

        n = first + UNITS
        put(first + 11, (V, G), "finish", b, 0)
        if b == B - 1:
            continue
        quick = b == B - 2
        put(n + 3, (V, G), "finish", b, 1)
        put(n + 5, (T,), "residual", b)
        put(n + 5, (V, G), "residual", b)
        put(n + 6, (V,), "norm", b)
        put(n + 7, (T, A), "normed", b)
        put(n + 8, (V,), "normed", b)
        for i in range(4):
            put(n + 9 + i, (T, A), "gate", b, i)
        put(n + 13, (A,), "silu", b)
        for i in range(4):
            put(n + 13 + i // (1 + quick), (T,), "up", b, i)
            put(n + 14 + i // (1 + quick), (V,), "up", b, i)
        if quick:
            put(n + 15, (A,), "compare", b, 0)
            continue
        for c in range(IC):
            k = n + 16 + 2 * c
            put(k, (A,), "compare", b, c)
            put(k + 1, (V,), "compare", b, c)
            put(k + 2, (T,), "wins", b, c, 0)
            put(k + 2, (T,), "wins", b, c, 1)
            put(k + 2, (V,), "wins", b, c, 0)
            put(k + 2, (V,), "wins", b, c, 1)
        for i in range(4):
            put(n + 22 + i, (T,), "down", b, i // 2, i % 2)
        put(n + 25, (V, S), "result", b, None)
    for n in range(B * UNITS):
        steps.append((ALL, ("unit", n // UNITS, n % UNITS)))
        steps += front[n] + behind[n]
    last = B - 1
    before = last - 1
    steps += [((V,), ("compare", before, 0)), ((T,), ("flush",)), ((V, G), ("finish", last, 1)), ((A,), ("compare", before, 1)),
              ((T,), ("wins", before, 0, 0)), ((T,), ("wins", before, 0, 1)), ((V,), ("wins", before, 0, 0)),
              ((V,), ("wins", before, 0, 1)), ((T, V, G), ("residual", last)), ((A, V), ("norm", last)),
              ((V,), ("compare", before, 1)), ((T, A, V), ("normed", last)),
              ((T,), ("wins", before, 1, 0)), ((T,), ("wins", before, 1, 1)), ((V,), ("wins", before, 1, 0)),
              ((V,), ("wins", before, 1, 1))]
    steps += [(ALL, ("gate", last, i)) for i in (0, 1)] + [(ALL, ("up", last, i)) for i in (0, 1)]
    steps += [((A, V), ("compare", last, 0))]
    steps += [((T,), ("down", before, tt, c)) for tt in range(2) for c in range(IC)] + [((V, S), ("result", before, None))]
    steps += [(ALL, ("gate", last, i)) for i in (2, 3)] + [(ALL, ("up", last, 2))]
    steps += [(ALL, ("wins", last, 0, pair)) for pair in range(2)] + [(ALL, ("up", last, 3)), ((A, V), ("compare", last, 1))]
    steps += [((T,), ("down", last, tt, 0)) for tt in range(2)]
    steps += [(ALL, ("wins", last, 1, pair)) for pair in range(2)]
    for tt in range(2):
        steps += [((T,), ("down", last, tt, 1)), ((V, S), ("result", last, tt))]
    return steps


def banks(steps):
    used, at = [[] for _ in range(WORK + 4)], {}
    for engines, s in steps:
        kind = s[0]
        if T not in engines:
            continue
        if kind in ("x_dbl", "bc") and s[1] == 0:
            keys, bank = [s], 1
        elif kind in ("context", "x_dbl", "step", "bc") or (kind == "conv" and s[2] == 0):
            keys, bank = [s[:2] if kind == "conv" else s], 2
        elif kind == "project":
            keys, bank = [("project", i) for i in range(3)], 0
        elif kind in ("residual", "normed"):
            keys, bank = [s], 0
        elif kind in ("gate", "up"):
            keys, bank = [s], s[2] % 2 + (2 if kind == "up" and s[1] == B - 1 else 0)
        elif kind == "wins":
            keys, bank = [s], s[3]
        elif kind == "taps":
            keys, bank = [("taps", i) for i in range(2)], 0
        elif kind == "down" and s[1] == B - 1 and s[3] == 0:
            keys, bank = [s[:3]], 4 + s[2]
        elif kind == "down" and s[1] < B - 1 and s[2:] == (0, 0):
            keys, bank = [s[:2]], 6 if s[1] == B - 2 else 1
        else:
            continue
        for i, key in enumerate(keys):
            n = bank + i % 2 if kind in ("taps", "project") else bank
            at[key] = (n, len(used[n]), used[n][-1] if used[n] else None)
            used[n].append(key)
    return at


def group(k, half):
    within = k % (UNITS // C)
    quad = 2 * (within % 2) + half
    return quad * SETS + within // 2, quad


def gated_block(nc, x, ctx_in, g_mix, g_ffn, in_w, conv_w, conv_b, xproj_w, step_w, step_b, a_log, skip,
                w_gate, w_up, w_down, out):
    F32, BF16, F32R = mybir.dt.float32, mybir.dt.bfloat16, mybir.dt.float32r
    ALU, ACT = mybir.AluOpType, mybir.ActivationFunctionType
    STEPS = order()
    BANK = banks(STEPS)

    with ExitStack() as stack:
        def sb(name, shape, dt=F32):
            return stack.enter_context(nc.sbuf_tensor(name, shape, dt))

        def sem(name):
            return stack.enter_context(nc.semaphore(name))

        x_sb = sb("x_sb", [P, B, C, L])
        ctx_sb = sb("ctx_sb", [P, B, C, D_CTX])
        in_w_sb = sb("in_w_sb", [P, C, D_CTX])
        conv_w_sb = sb("conv_w_sb", [P, C, TAPS])
        conv_b_sb = sb("conv_b_sb", [P, C])
        step_b_sb = sb("step_b_sb", [P, C])
        skip_sb = sb("skip_sb", [P, C])
        xproj_sb = sb("xproj_sb", [DR + 2 * NS, D_IN])
        step_w_sb = sb("step_w_sb", [P, C, DR])
        a_log_sb = sb("a_log_sb", [GROUPS, P])
        gains_sb = sb("gains_sb", [P, 2])
        up_raw = sb("up_raw", [P, KB, 2, HID])
        down_sb = sb("down_sb", [P, IC, 4, D_IN])
        ident = sb("ident", [P, P])
        plus_b = sb("plus_b", [P, P], BF16)
        minus_b = sb("minus_b", [P, P], BF16)
        spread_r = sb("spread_r", [P, ES, P], F32R)
        spread_bc_f = sb("spread_bc_f", [4 * NS, 2, P])
        spread_bc = sb("spread_bc", [4 * NS, 2, P], F32R)
        warm = sb("warm", [P, P], BF16)
        gather = sb("gather", [P, SETS, 32])
        power = sb("power", [P, C])
        in_taps = sb("in_taps", [P, TAPS, D_IN])
        xproj_t = sb("xproj_t", [P, C, DR + 2 * NS])
        step_wt = sb("step_wt", [DR, D_IN])
        a_exp = sb("a_exp", [P, GROUPS])
        a_neg = sb("a_neg", [P, GROUPS])
        gains = sb("gains", [P, 2])
        up_hi = sb("up_hi", [P, KB, 2, 4, D_IN], F32R)
        up_lo = sb("up_lo", [P, KB, 2, 4, D_IN], F32R)
        ctx_t = sb("ctx_t", [P, 2, TAPS - 1 + L])
        stats = sb("stats", [P, B, C, 6])
        moments = sb("moments", [P, B, C, 2])
        veps = sb("veps", [P, B, C])
        rstd = sb("rstd", [P, B, C])
        shift = sb("shift", [P, B, C])
        z_gate = sb("z_gate", [P, 2, C, L])
        u = sb("u", [P, 3, C, L])
        bc_parts = sb("bc_parts", [4 * NS, L], F32R)
        bc = sb("bc", [P, 2, 2, L])
        low = sb("low", [DR, 2, L])
        sp_abs = sb("sp_abs", [P, C, L])
        sp_exp = sb("sp_exp", [P, C, L])
        sp_pos = sb("sp_pos", [P, C, L])
        sp_ln = sb("sp_ln", [P, C, L])
        sp_back = sb("sp_back", [P, C, L])
        sp_lost = sb("sp_lost", [P, C, L])
        du_parts = sb("du_parts", [P, 2, C, L], F32R)
        delta = sb("delta", [P, C, L])
        du = sb("du", [P, C, L])
        delta_h = sb("delta_h", [P, 2, 2, C, L], F32R)
        du_h = sb("du_h", [P, 2, 2, C, L], F32R)
        decay = sb("decay", [P, N_DECAY, 2, L])
        state = sb("state", [P, N_STATE, 2, L])
        prod = sb("prod", [P, N_PROD, 2, L])
        mixed = sb("mixed", [P, C, L])
        x2 = x_sb
        stats2 = sb("stats2", [P, B, C, 6])
        moments2 = sb("moments2", [P, B, C, 2])
        veps2 = sb("veps2", [P, B, C])
        rstd2 = sb("rstd2", [P, B, C])
        xn = sb("xn", [P, C, L])
        xnt_hi = sb("xnt_hi", [P, KB, L], F32R)
        xnt_lo = sb("xnt_lo", [P, KB, L], F32R)
        gate_s = up_raw[:, 0].rearrange("p w (j t) -> p w j t", j=4)
        h = sb("h", [P, IC, 4, L])
        taps_d = h[:, 0].rearrange("p (c j) (k q) -> p c (j k) q", c=C, q=P)
        spread_f = h[:, 1].rearrange("p j (k q) -> p (j k) q", q=P)
        h_abs = up_raw[:, 1].rearrange("p w (j t) -> p w j t", j=4)
        beats = sb("beats", [P, IC, 6, L], BF16)
        h_kept = sb("h_kept", [P, IC, 4, L])
        result = sb("result", [P, 2, C, L])

        dec_ps = [stack.enter_context(nc.psum_tensor(f"dec_ps{i}", [P, 2, L], F32)) for i in range(2)]
        drv_ps = [stack.enter_context(nc.psum_tensor(f"drv_ps{i}", [P, 2, L], F32)) for i in range(2)]
        y_ps = stack.enter_context(nc.psum_tensor("y_ps", [P, C, L], F32))
        work = [stack.enter_context(nc.psum_tensor(f"work{i}", [P, 2, L], F32)) for i in range(WORK)]
        work += drv_ps + dec_ps

        ctx_loaded = [sem(f"ctx_loaded{b}") for b in range(B)]
        x_loaded = [sem(f"x_loaded{b}") for b in range(B)]
        taps_loaded, proj_loaded, small_loaded = sem("taps_loaded"), sem("proj_loaded"), sem("small_loaded")
        up_loaded, down_loaded = sem("up_loaded"), sem("down_loaded")
        stored = [sem(f"stored{b}") for b in range(B)]
        warm_ready, blank, masks_ready, pads_ready = sem("warm_ready"), sem("blank"), sem("masks_ready"), sem("pads_ready")
        masks_cast, diags_ready, taps_ready = sem("masks_cast"), sem("diags_ready"), sem("taps_ready")
        project_ready, a_raw, a_ready, gains_ready = sem("project_ready"), sem("a_raw"), sem("a_ready"), sem("gains_ready")
        hi_ready, lo_ready = sem("hi_ready"), sem("lo_ready")
        filled = [sem(f"filled{i}") for i in range(WORK + 4)]
        ctx_turned = sem("ctx_turned")
        x_stats, x_moments, x_veps, x_rstd, x_shift = (sem(n) for n in ("x_stats", "x_moments", "x_veps", "x_rstd", "x_shift"))
        u_ready, z_ready, bc_hi, bc_lo, bc_ready, low_ready = (
            sem(n) for n in ("u_ready", "z_ready", "bc_hi", "bc_lo", "bc_ready", "low_ready"))
        abs_ready, pos_ready, exp_ready, ln_ready = (sem(n) for n in ("abs_ready", "pos_ready", "exp_ready", "ln_ready"))
        back_ready, lost_ready, sum_ready, delta_ready, du_ready = (
            sem(n) for n in ("back_ready", "lost_ready", "sum_ready", "delta_ready", "du_ready"))
        delta_hi, delta_lo, du_hi, du_lo = (sem(n) for n in ("delta_hi", "delta_lo", "du_hi", "du_lo"))
        du_moved = sem("du_moved")
        zero_col = sem("zero_col")
        delta_spread, du_spread, decay_ready, drive_ready, scanned, prod_ready, summed = (
            sem(n) for n in ("delta_spread", "du_spread", "decay_ready", "drive_ready", "scanned", "prod_ready", "summed"))
        skip_added, mixed_ready, x2_ready = sem("skip_added"), sem("mixed_ready"), sem("x2_ready")
        s_stats, s_moments, s_veps, s_rstd, xn_ready = (sem(n) for n in ("s_stats", "s_moments", "s_veps", "s_rstd", "xn_ready"))
        xnt_hi_ready, xnt_lo_ready, gate_out, gate_ready, h_ready, h_abs_ready = (
            sem(n) for n in ("xnt_hi_ready", "xnt_lo_ready", "gate_out", "gate_ready", "h_ready", "h_abs_ready"))
        beats_ready, kept_ready, result_ready = (
            sem(n) for n in ("beats_ready", "kept_ready", "result_ready"))

        block = stack.enter_context(nc.Block())

        def steps_of(engine):
            return [step for engines, step in STEPS if engine in engines]

        def has(eng, key):
            n, before, _ = BANK[key]
            eng.wait_ge(filled[n], before + 1)
            return work[n]

        def last_read(key):
            kind, b = key[0], key[1]
            if kind == "wins":
                return kept_ready, 8 * b + 4 * key[2] + 2 * key[3] + 2
            return {
                "taps": lambda: (taps_ready, b + 1), "project": lambda: (project_ready, b + 1),
                "context": lambda: (ctx_turned, b + 1), "conv": lambda: (u_ready, b + 1),
                "bc": lambda: (bc_ready, b + 1), "x_dbl": lambda: (bc_lo, b + 1),
                "step": lambda: (pos_ready, b + 1), "residual": lambda: (x2_ready, C * (b + 1)),
                "normed": lambda: (xnt_lo_ready, b + 1), "gate": lambda: (gate_ready if b == B - 1 else gate_out, 4 * b + key[2] + 1),
                "up": lambda: (h_ready, 4 * b + key[2] + 1), "down": lambda: (result_ready, C * (b + 1) if len(key) == 2 else C * b + key[2] + 1),
            }[kind]()

        def direct(b, which):
            return which == 0 or b == 0

        def index(b, k):
            return UNITS * b + k

        @block.sync
        def _(sp):
            sp.dma_start(in_w_sb[:], in_w.rearrange("(c p) d -> p c d", p=P)).then_inc(taps_loaded, 16)
            sp.dma_start(conv_w_sb[:], conv_w.rearrange("(c p) k -> p c k", p=P)).then_inc(taps_loaded, 16)
            sp.dma_start(ctx_sb[:, 0], ctx_in[0].rearrange("(c p) d -> p c d", p=P)).then_inc(ctx_loaded[0], 16)
            sp.dma_start(xproj_sb[:], xproj_w).then_inc(proj_loaded, 16)
            sp.dma_start(step_w_sb[:], step_w.rearrange("(c p) r -> p c r", p=P)).then_inc(proj_loaded, 16)
            sp.dma_start(a_log_sb[:], a_log.rearrange("(g e) n -> g (e n)", e=ES)).then_inc(proj_loaded, 16)
            for dst, src in ((conv_b_sb, conv_b), (step_b_sb, step_b), (skip_sb, skip)):
                sp.dma_start(dst[:], src.rearrange("(c p) -> p c", p=P), allow_slow_non_contiguous=True).then_inc(small_loaded, 16)
            sp.dma_start(gains_sb[:, 0:1], g_mix[None, :].broadcast_to([P, 1])).then_inc(small_loaded, 16)
            sp.dma_start(gains_sb[:, 1:2], g_ffn[None, :].broadcast_to([P, 1])).then_inc(small_loaded, 16)
            sp.dma_start(x_sb[:, 0], x[0].rearrange("(c p) d -> p c d", p=P)).then_inc(x_loaded[0], 16)
            for b in range(1, B):
                sp.dma_start(ctx_sb[:, b], ctx_in[b].rearrange("(c p) d -> p c d", p=P)).then_inc(ctx_loaded[b], 16)
                sp.dma_start(x_sb[:, b], x[b].rearrange("(c p) d -> p c d", p=P)).then_inc(x_loaded[b], 16)
            sp.dma_start(up_raw[:, :, 0], w_gate.rearrange("(k p) i -> p k i", p=P)).then_inc(up_loaded, 16)
            sp.dma_start(up_raw[:, :, 1], w_up.rearrange("(k p) i -> p k i", p=P)).then_inc(up_loaded, 16)
            sp.dma_start(down_sb[:], w_down.rearrange("(c p j) n -> p c j n", p=P, j=4)).then_inc(down_loaded, 16)
            for step in steps_of(S):
                if step[0] == "halves":
                    b = step[1]
                    if b >= 2:
                        sp.wait_ge(du_spread, UNITS * (b - 1))
                    for part, ready in ((0, du_hi), (1, du_lo)):
                        sp.wait_ge(ready, b + 2)
                        for q in range(2):
                            to = 64 * (q ^ part)
                            sp.dma_start(du_h[to:to + 64, b % 2, q].bitcast(F32),
                                         du_parts[64 * q:64 * q + 64, part].bitcast(F32)).then_inc(du_moved, 16)
                elif step[0] == "result":
                    _, b, tt = step
                    if tt is None:
                        sp.wait_ge(result_ready, C * (b + 1))
                        sp.dma_start(out[b].rearrange("(c p) d -> p c d", p=P), result[:, b % 2]).then_inc(stored[b], 16)
                    else:
                        sp.wait_ge(result_ready, C * b + tt + 1)
                        sp.dma_start(out[b, tt * P:(tt + 1) * P], result[:, b % 2, tt]).then_inc(stored[b], 16)
            for b in range(B):
                sp.wait_ge(stored[b], 16 if b < B - 1 else 32)

        @block.gpsimd
        def _(pool):
            for step in steps_of(G):
                kind, b = step[0], step[1] if len(step) > 1 else None
                if kind == "masks":
                    pool.memset(warm[:], 0.0).then_inc(warm_ready, 1)
                    pool.memset(ident[:], 0.0).then_inc(blank, 1)
                    pool.memset(ctx_t[:, :, 0:TAPS - 1], 0.0).then_inc(pads_ready, 1)
                    pool.memset(spread_f[:], 0.0).then_inc(blank, 1)
                    pool.memset(spread_bc_f[:], 0.0).then_inc(blank, 1)
                    pool.memset(gather[:], 1.0).then_inc(blank, 1)
                    pool.memset(power[:], -0.5).then_inc(pads_ready, 1)
                    pool.memset(decay[:, :, :, 0:1], 0.0).then_inc(zero_col, 1)
                    pool.wait_ge(blank, 4)
                    pool.affine_select(out=ident[:], in_=ident[:], compare_op=ALU.not_equal, fill=1.0, base=0,
                                       pattern=[[-1, P]], channel_multiplier=1).then_inc(masks_ready, 1)
                    wide = spread_f[:].rearrange("p g (e n) -> p g e n", n=NS)
                    for rows, base in ((0, 0), (1, -64)):
                        pool.affine_select(out=wide, in_=wide, compare_op=ALU.not_equal, fill=1.0, base=base,
                                           pattern=[[-ES, ES], [-1, ES], [0, NS]],
                                           channel_multiplier=1).then_inc(masks_ready, 1)
                        pool.wait_ge(masks_ready, 2 + rows)
                    wide = spread_bc_f[:].rearrange("p i (e n) -> p i e n", n=NS)
                    for rows, base in ((0, 0), (1, -2 * NS)):
                        pool.affine_select(out=wide, in_=wide, compare_op=ALU.not_equal, fill=1.0, base=base,
                                           pattern=[[-NS, 2], [0, ES], [-1, NS]],
                                           channel_multiplier=1).then_inc(masks_ready, 1)
                        pool.wait_ge(masks_ready, 4 + rows)
                    pool.affine_select(out=gather[:], in_=gather[:], compare_op=ALU.is_ge, fill=0.0, base=0,
                                       pattern=[[P, SETS], [-NS, 32]], channel_multiplier=1).then_inc(masks_ready, 1)
                    pool.wait_ge(masks_ready, 6)
                    pool.affine_select(out=gather[:], in_=gather[:], compare_op=ALU.is_ge, fill=0.0, base=NS - 1,
                                       pattern=[[-P, SETS], [NS, 32]], channel_multiplier=-1).then_inc(masks_ready, 1)
                elif kind == "context":
                    pool.wait_ge(pads_ready, 2)
                    pool.wait_ge(x_veps, b + 1)
                    pool.tensor_tensor(rstd[:, b], veps[:, b], power[:], ALU.pow).then_inc(x_rstd, 1)
                elif kind == "split_up":
                    k, w = divmod(step[1], 2)
                    if step[1] % 2:
                        continue
                    pool.wait_ge(hi_ready, step[1] + 1)
                    pool.tensor_tensor(up_lo[:, k, w], up_raw[:, k, w].rearrange("p (g j) -> p j g", j=4),
                                       up_hi[:, k, w].bitcast(F32), ALU.subtract).then_inc(lo_ready, 1)
                elif kind == "softplus":
                    pool.wait_ge(pos_ready, b + 1)
                    pool.wait_ge(lost_ready, b + 1)
                    pool.tensor_tensor(sp_abs[:], sp_pos[:], sp_lost[:], ALU.add).then_inc(sum_ready, 1)
                elif kind == "delta" and b:
                    pool.wait_ge(ln_ready, b + 1)
                    pool.wait_ge(sum_ready, b + 1)
                    pool.wait_ge(delta_hi, 2 * b)
                    pool.wait_ge(delta_lo, 2 * b)
                    pool.tensor_tensor(delta[:], sp_abs[:], sp_ln[:], ALU.add).then_inc(delta_ready, 1)
                    pool.wait_ge(delta_ready, b + 1)
                    pool.wait_ge(du_hi, b + 1)
                    pool.wait_ge(du_lo, b + 1)
                    pool.tensor_tensor(du[:], delta[:], u[:, b % 3], ALU.mult).then_inc(du_ready, 1)
                elif kind == "unit":
                    n = index(*step[1:])
                    pool.wait_ge(scanned, n + 1)
                    pool.wait_ge(bc_ready, b + 1)
                    if n >= N_PROD:
                        pool.wait_ge(summed, (n - N_PROD) // 2 + 1)
                    pool.tensor_tensor(prod[:, n % N_PROD], state[:, n % N_STATE],
                                       bc[:, b % 2, 1:2].broadcast_to([P, 2, L]), ALU.mult).then_inc(prod_ready, 1)
                elif kind == "finish":
                    n = C * b + step[2]
                    pool.wait_ge(skip_added, n + 1)
                    pool.wait_ge(z_ready, b + 1)
                    pool.tensor_tensor(mixed[:, step[2]], mixed[:, step[2]], z_gate[:, b % 2, step[2]],
                                       ALU.mult).then_inc(mixed_ready, 1)
                elif kind == "residual":
                    pool.wait_ge(s_veps, b + 1)
                    pool.tensor_tensor(rstd2[:, b], veps2[:, b], power[:], ALU.pow).then_inc(s_rstd, 1)

        @block.scalar
        def _(act):
            def decay_of(n):
                b, k = divmod(n, UNITS)
                act.wait_ge(delta_spread, n + 1)
                if n == 0:
                    act.wait_ge(zero_col, 1)
                if n >= N_DECAY:
                    act.wait_ge(scanned, n - N_DECAY + 1)
                for half in range(2):
                    g, _ = group(k, half)
                    col = (k // (UNITS // C)) * (GROUPS // C) + g
                    last = act.activation(decay[:, n % N_DECAY, half, 1:L], dec_ps[n % 2][:, half, 1:L], ACT.Exp,
                                          scale=a_neg[:, col:col + 1])
                last.then_inc(decay_ready, 1)

            for step in steps_of(A):
                kind, b = step[0], step[1] if len(step) > 1 else None
                if kind == "load":
                    act.preload_act_table_set("silu_and_others")
                elif kind == "masks":
                    act.wait_ge(masks_ready, 7)
                    act.activation(spread_r[:], spread_f[:], ACT.Copy).then_inc(masks_cast, 1)
                    act.activation(spread_bc[:], spread_bc_f[:], ACT.Copy).then_inc(masks_cast, 1)
                    act.activation(plus_b[:], ident[:], ACT.Copy).then_inc(masks_cast, 1)
                    act.activation(minus_b[:], ident[:], ACT.Copy, scale=-1.0).then_inc(masks_cast, 1)
                elif kind == "taps":
                    for i in range(2):
                        bank = has(act, ("taps", i))
                        act.activation(in_taps[:, 2 * i:2 * i + 2, :], bank[:], ACT.Copy).then_inc(taps_ready, 1)
                elif kind == "project":
                    act.wait_ge(project_ready, 2)
                    bank = has(act, ("project", 2))
                    act.activation(a_exp[:], bank[:, 0, 0:GROUPS], ACT.Copy).then_inc(project_ready, 1)
                elif kind == "context":
                    bank = has(act, step)
                    if b:
                        act.wait_ge(pads_ready, 1)
                    if b >= 2:
                        has(act, ("conv", b - 2))
                    act.activation(ctx_t[:, b % 2, TAPS - 1:], bank[:].rearrange("p a t -> p (a t)")[:, 0:L],
                                   ACT.Copy).then_inc(ctx_turned, 1)
                elif kind == "gate_in":
                    act.preload_act_table_set("silu_and_others")
                    if b == 0:
                        act.wait_ge(small_loaded, 16 * 5)
                        act.activation(gains[:], gains_sb[:], ACT.Tanh).then_inc(gains_ready, 1)
                    bank = has(act, ("conv", b))
                    if b >= 3:
                        act.wait_ge(mixed_ready, C * (b - 2))
                    for c in range(C):
                        last = act.activation(u[:, b % 3, c], bank[:, c], ACT.Silu, bias=conv_b_sb[:, c:c + 1])
                    last.then_inc(u_ready, 1)
                    act.preload_act_table_set("natural_log_exp_and_others")
                elif kind == "bc":
                    bank = has(act, step)
                    if b >= 2:
                        act.wait_ge(scanned, UNITS * (b - 1))
                        act.wait_ge(prod_ready, UNITS * (b - 1))
                    act.activation(bc[:, b % 2], bank[:], ACT.Copy).then_inc(bc_ready, 1)
                elif kind == "softplus":
                    bank = has(act, ("step", b))
                    if b:
                        act.wait_ge(exp_ready, b)
                        act.wait_ge(lost_ready, b)
                        act.wait_ge(sum_ready, b)
                        act.wait_ge(delta_ready, b)
                    for c in range(C):
                        last = act.activation(sp_abs[:, c], bank[:, c], ACT.Abs, bias=step_b_sb[:, c:c + 1])
                    last.then_inc(abs_ready, 1)
                    act.wait_ge(abs_ready, b + 1)
                    act.activation(sp_exp[:], sp_abs[:], ACT.Exp, scale=-1.0).then_inc(exp_ready, 1)
                    act.wait_ge(exp_ready, b + 1)
                    act.activation(sp_ln[:], sp_exp[:], ACT.Ln, bias=1.0).then_inc(ln_ready, 1)
                    for c in range(C):
                        last = act.activation(sp_pos[:, c], bank[:, c], ACT.Relu, bias=step_b_sb[:, c:c + 1])
                    last.then_inc(pos_ready, 1)
                elif kind == "halves":
                    src, ready, done = ((delta, delta_ready, delta_hi), (du, du_ready, du_hi))[step[2]]
                    act.wait_ge(ready, b + 1)
                    if direct(*step[1:]):
                        if b >= 2:
                            act.wait_ge(delta_spread, UNITS * (b - 1))
                        for q in range(2):
                            rows = slice(64 * q, 64 * q + 64)
                            act.activation((delta_h, du_h)[step[2]][rows, b % 2, q], src[rows], ACT.Copy).then_inc(done, 1)
                    else:
                        if b >= 2:
                            act.wait_ge(du_moved, 64 * (b - 1))
                        act.activation(du_parts[:, 0], src[:], ACT.Copy).then_inc(done, 1)
                elif kind == "tables":
                    act.wait_ge(project_ready, 3)
                    act.activation(a_neg[:], a_exp[:], ACT.Exp).then_inc(a_raw, 1)
                    act.wait_ge(a_raw, 1)
                    act.activation(a_exp[:], a_neg[:], ACT.Copy, scale=-1.0).then_inc(a_raw, 1)
                    act.wait_ge(a_raw, 2)
                    act.activation(a_neg[:], a_exp[:], ACT.Copy).then_inc(a_ready, 1)
                    act.wait_ge(a_ready, 1)
                elif kind == "ahead":
                    for n in range(SPREAD_AHEAD - 1):
                        decay_of(n)
                elif kind == "unit":
                    n = index(*step[1:]) + SPREAD_AHEAD - 1
                    if n < UNITS * B:
                        decay_of(n)
                elif kind == "split_up":
                    k, w = divmod(step[1], 2)
                    act.wait_ge(up_loaded, 32)
                    act.activation(up_hi[:, k, w], up_raw[:, k, w].rearrange("p (g j) -> p j g", j=4),
                                   ACT.Copy).then_inc(hi_ready, 1)
                elif kind == "norm":
                    act.preload_act_table_set("silu_and_others")
                elif kind == "normed":
                    bank = has(act, step)
                    if b:
                        has(act, ("up", b - 1, 3))
                    act.activation(xnt_hi[:], bank[:], ACT.Copy).then_inc(xnt_hi_ready, 1)
                elif kind == "gate":
                    i = step[2]
                    bank = has(act, step)
                    if b:
                        act.wait_ge(h_ready, 4 * (b - 1) + i + 1)
                    last = b == B - 1
                    act.activation(gate_s[:, i // 2, 2 * (i % 2):2 * (i % 2) + 2], bank[:],
                                   ACT.Silu if last else ACT.Copy).then_inc(gate_ready if last else gate_out, 1)
                elif kind == "silu":
                    act.preload_act_table_set("silu_and_others")
                    for z in {-1: (0, 1), B - 2: ()}.get(b, (b + 2,)):
                        act.wait_ge(x_shift, z + 1)
                        if z >= 2:
                            act.wait_ge(mixed_ready, C * (z - 1))
                        for c in range(C):
                            last = act.activation(z_gate[:, z % 2, c], x_sb[:, z, c], ACT.Silu,
                                                  bias=shift[:, z, c:c + 1], scale=rstd[:, z, c:c + 1])
                        last.then_inc(z_ready, 1)
                    for i in range(4 if b >= 0 else 0):
                        act.wait_ge(gate_out, 4 * b + i + 1)
                        act.activation(gate_s[:, i // 2, 2 * (i % 2):2 * (i % 2) + 2],
                                       gate_s[:, i // 2, 2 * (i % 2):2 * (i % 2) + 2], ACT.Silu).then_inc(gate_ready, 1)
                    act.preload_act_table_set("natural_log_exp_and_others")
                elif kind == "compare":
                    c = step[2]
                    act.wait_ge(h_ready, 4 * b + 2 * c + 2)
                    if b:
                        act.wait_ge(beats_ready, 3 * (2 * (b - 1) + c + 1))
                    act.activation(h_abs[:, c], h[:, c], ACT.Abs).then_inc(h_abs_ready, 1)

        @block.vector
        def _(dve):
            for step in steps_of(V):
                kind, b = step[0], step[1] if len(step) > 1 else None
                if kind == "taps":
                    dve.wait_ge(taps_loaded, 32)
                    dve.wait_ge(masks_ready, 1)
                    for c in range(C):
                        for k in range(TAPS):
                            last = dve.tensor_scalar(taps_d[:, c, k], ident[:], conv_w_sb[:, c, k:k + 1], None, ALU.mult)
                        last.then_inc(diags_ready, 1)
                elif kind == "project":
                    bank = has(dve, ("project", 0))
                    W = DR + 2 * NS
                    dve.tensor_copy(xproj_t[:, :, 0:2 * NS], bank[:, :, DR:W])
                    dve.tensor_copy(xproj_t[:, :, 2 * NS:W], bank[:, :, 0:DR]).then_inc(project_ready, 1)
                    bank = has(dve, ("project", 1))
                    dve.tensor_copy(step_wt[:], bank[0:DR].rearrange("p a t -> p (a t)")[:, 0:D_IN]).then_inc(project_ready, 1)
                elif kind == "context":
                    dve.wait_ge(x_loaded[b], 16)
                    for c in range(C):
                        dve.bn_stats(stats[:, b, c], x_sb[:, b, c]).then_inc(x_stats, 1)
                    for c in range(C):
                        dve.wait_ge(x_stats, C * b + c + 1)
                        dve.bn_aggr(moments[:, b, c], stats[:, b, c]).then_inc(x_moments, 1)
                    dve.wait_ge(x_moments, C * (b + 1))
                    dve.tensor_scalar(veps[:, b], moments[:, b, :, 1], EPS, None, ALU.add).then_inc(x_veps, 1)
                elif kind == "shift":
                    dve.wait_ge(x_rstd, b + 1)
                    dve.scalar_tensor_tensor(shift[:, b], moments[:, b, :, 0], -1.0, rstd[:, b], ALU.mult,
                                             ALU.mult).then_inc(x_shift, 1)
                elif kind == "x_dbl":
                    bank = has(dve, step)
                    dve.tensor_copy(low[:, b % 2], bank[2 * NS:2 * NS + DR, 0]).then_inc(low_ready, 1)
                    if b:
                        dve.wait_ge(bc_ready, b)
                    dve.tensor_copy(bc_parts[0:2 * NS], bank[0:2 * NS, 0]).then_inc(bc_hi, 1)
                    dve.wait_ge(bc_hi, b + 1)
                    dve.tensor_tensor(bc_parts[2 * NS:4 * NS], bank[0:2 * NS, 0], bc_parts[0:2 * NS].bitcast(F32),
                                      ALU.subtract).then_inc(bc_lo, 1)
                elif kind == "split_up" and step[1] % 2:
                    k, w = divmod(step[1], 2)
                    dve.wait_ge(hi_ready, step[1] + 1)
                    dve.tensor_tensor(up_lo[:, k, w], up_raw[:, k, w].rearrange("p (g j) -> p j g", j=4),
                                      up_hi[:, k, w].bitcast(F32), ALU.subtract).then_inc(lo_ready, 1)
                elif kind == "softplus":
                    dve.wait_ge(exp_ready, b + 1)
                    dve.tensor_scalar(sp_back[:], sp_exp[:], 1.0, 1.0, ALU.add, ALU.subtract).then_inc(back_ready, 1)
                    dve.wait_ge(back_ready, b + 1)
                    if b:
                        dve.wait_ge(sum_ready, b)
                    dve.tensor_tensor(sp_lost[:], sp_exp[:], sp_back[:], ALU.subtract).then_inc(lost_ready, 1)
                elif kind == "delta" and b == 0:
                    dve.wait_ge(ln_ready, b + 1)
                    dve.wait_ge(sum_ready, b + 1)
                    dve.tensor_tensor(delta[:], sp_abs[:], sp_ln[:], ALU.add).then_inc(delta_ready, 1)
                    dve.wait_ge(delta_ready, 1)
                    dve.tensor_tensor(du[:], delta[:], u[:, 0], ALU.mult).then_inc(du_ready, 1)
                elif kind == "halves":
                    src, hi, done = ((delta, delta_hi, delta_lo), (du, du_hi, du_lo))[step[2]]
                    if direct(*step[1:]):
                        dst = (delta_h, du_h)[step[2]]
                        for q in range(2):
                            dve.wait_ge(hi, 2 * b + q + 1)
                            rows, other = slice(64 * q, 64 * q + 64), slice(64 - 64 * q, 128 - 64 * q)
                            dve.tensor_tensor(dst[other, b % 2, q], src[rows], dst[rows, b % 2, q].bitcast(F32),
                                              ALU.subtract).then_inc(done, 1)
                    else:
                        dve.wait_ge(hi, b + 2)
                        dve.tensor_tensor(du_parts[:, 1], src[:], du_parts[:, 0].bitcast(F32), ALU.subtract).then_inc(done, 1)
                elif kind == "unit":
                    n = index(*step[1:])
                    dve.wait_ge(du_spread, n + 1)
                    dve.wait_ge(bc_ready, b + 1)
                    drive = drv_ps[n % 2]
                    dve.tensor_tensor(drive[:], drive[:], bc[:, b % 2, 0:1].broadcast_to([P, 2, L]),
                                      ALU.mult).then_inc(drive_ready, 1)
                    dve.wait_ge(drive_ready, n + 1)
                    dve.wait_ge(decay_ready, n + 1)
                    if n >= N_STATE:
                        dve.wait_ge(prod_ready, n - N_STATE + 1)
                    dve.tensor_tensor_scan(state[:, n % N_STATE].rearrange("p a t -> p (a t)"),
                                           decay[:, n % N_DECAY].rearrange("p a t -> p (a t)"),
                                           drive[:].rearrange("p a t -> p (a t)"), 0.0, ALU.mult,
                                           ALU.add).then_inc(scanned, 1)
                elif kind == "finish":
                    c = step[2]
                    n = C * b + c
                    dve.wait_ge(summed, UNITS // 2 // C * (n + 1))
                    dve.wait_ge(u_ready, b + 1)
                    if b:
                        has(dve, ("residual", b - 1))
                    dve.scalar_tensor_tensor(mixed[:, c], u[:, b % 3, c], skip_sb[:, c:c + 1], y_ps[:, c], ALU.mult,
                                             ALU.add).then_inc(skip_added, 1)
                elif kind == "residual":
                    bank = has(dve, step)
                    dve.wait_ge(gains_ready, 1)
                    dve.wait_ge(x_loaded[b], 16)
                    for c in range(C):
                        last = dve.scalar_tensor_tensor(x2[:, b, c], bank[:, c], gains[:, 0:1], x_sb[:, b, c],
                                                        ALU.mult, ALU.add)
                        last.then_inc(x2_ready, 1)
                    dve.wait_ge(x2_ready, C * (b + 1))
                    for c in range(C):
                        dve.bn_stats(stats2[:, b, c], x2[:, b, c]).then_inc(s_stats, 1)
                    for c in range(C):
                        dve.wait_ge(s_stats, C * b + c + 1)
                        dve.bn_aggr(moments2[:, b, c], stats2[:, b, c]).then_inc(s_moments, 1)
                    dve.wait_ge(s_moments, C * (b + 1))
                    dve.tensor_scalar(veps2[:, b], moments2[:, b, :, 1], EPS, None, ALU.add).then_inc(s_veps, 1)
                elif kind == "norm":
                    dve.wait_ge(s_rstd, b + 1)
                    if b:
                        has(dve, ("normed", b - 1))
                    for c in range(C):
                        dve.tensor_scalar(xn[:, c], x2[:, b, c], moments2[:, b, c, 0:1], rstd2[:, b, c:c + 1],
                                          ALU.subtract, ALU.mult).then_inc(xn_ready, 1)
                elif kind == "normed":
                    bank = has(dve, step)
                    dve.wait_ge(xnt_hi_ready, b + 1)
                    dve.tensor_tensor(xnt_lo[:], bank[:], xnt_hi[:].bitcast(F32), ALU.subtract).then_inc(xnt_lo_ready, 1)
                elif kind == "up":
                    i = step[2]
                    bank = has(dve, step)
                    dve.wait_ge(gate_ready, 4 * b + i + 1)
                    if b:
                        dve.wait_ge(kept_ready, 8 * (b - 1) + 4 * (i // 2) + 4)
                        dve.wait_ge(h_abs_ready, 2 * (b - 1) + i // 2 + 1)
                    mem = slice(2 * (i % 2), 2 * (i % 2) + 2)
                    dve.tensor_tensor(h[:, i // 2, mem], gate_s[:, i // 2, mem], bank[:], ALU.mult).then_inc(h_ready, 1)
                elif kind == "compare":
                    c = step[2]
                    n = 2 * b + c
                    dve.wait_ge(h_abs_ready, n + 1)
                    if b:
                        has(dve, ("wins", b - 1, c, 1))
                    for at, m, d in ((0, 3, 1), (3, 2, 2), (5, 1, 3)):
                        dve.tensor_tensor(beats[:, c, at:at + m], h_abs[:, c, 0:m], h_abs[:, c, d:d + m],
                                          ALU.is_ge).then_inc(beats_ready, 1)
                elif kind == "wins":
                    _, _, c, pair = step
                    bank = has(dve, step)
                    dve.wait_ge(h_ready, 4 * b + 2 * c + 2)
                    if b:
                        has(dve, ("down", b - 1))
                    for m in range(2):
                        j = 2 * pair + m
                        last = dve.scalar_tensor_tensor(h_kept[:, c, j], bank[:, m], 1.5 - j, h[:, c, j],
                                                        ALU.is_ge, ALU.mult)
                        last.then_inc(kept_ready, 1)
                elif kind == "result":
                    tt = step[2]
                    bank = has(dve, ("down", b) if tt is None else ("down", b, tt))
                    if b >= 2:
                        dve.wait_ge(stored[b - 2], 16)
                    if tt is None:
                        dve.scalar_tensor_tensor(result[:, b % 2], bank[:], gains[:, 1:2], x2[:, b], ALU.mult,
                                                 ALU.add).then_inc(result_ready, C)
                    else:
                        dve.scalar_tensor_tensor(result[:, b % 2, tt], bank[:, 0], gains[:, 1:2], x2[:, b, tt], ALU.mult,
                                                 ALU.add).then_inc(result_ready, 1)

        @block.tensor
        def _(pe):
            def take(key):
                n, _, prior = BANK[key]
                if prior:
                    pe.wait_ge(*last_read(prior))
                return work[n]

            def spread(n, src, dst, ready):
                b, k = divmod(n, UNITS)
                c = k // (UNITS // C)
                for half in range(2):
                    g, quad = group(k, half)
                    last = pe.matmul(dst[n % 2][:, half], spread_r[:, g % ES], src[:, b % 2, quad // 2, c],
                                     start=True, stop=True)
                last.then_inc(ready, 1)

            def spread_delta(n):
                if n % UNITS == 0:
                    pe.wait_ge(delta_hi, 2 * (n // UNITS + 1))
                    pe.wait_ge(delta_lo, 2 * (n // UNITS + 1))
                if n >= 2:
                    pe.wait_ge(decay_ready, n - 1)
                spread(n, delta_h, dec_ps, delta_spread)

            def spread_du(n):
                if n % UNITS == 0:
                    if n == 0:
                        pe.wait_ge(du_hi, 2)
                        pe.wait_ge(du_lo, 2)
                    else:
                        pe.wait_ge(du_moved, 64 * (n // UNITS))
                if n >= 2:
                    pe.wait_ge(scanned, n - 1)
                spread(n, du_h, drv_ps, du_spread)

            def sum_states(s):
                b, r = divmod(s, UNITS // 2)
                c, r = divmod(r, SETS)
                pe.wait_ge(prod_ready, 2 * s + 2)
                if r == 0 and s >= SETS:
                    pe.wait_ge(skip_added, C * b + c)
                for quad in range(QUADS):
                    n = 2 * s + quad // 2
                    last = pe.matmul(y_ps[32 * quad:32 * quad + 32, c], gather[:, r], prod[:, n % N_PROD, quad % 2],
                                     start=(r == 0), stop=(r == SETS - 1), tile_position=(0, 32 * quad))
                last.then_inc(summed, 1)

            for step in steps_of(T):
                kind, b = step[0], step[1] if len(step) > 1 else None
                if kind == "load":
                    pe.wait_ge(warm_ready, 1)
                    for _ in range(WARM):
                        pe.matmul(work[0][:, 0, 0:P], warm[:], warm[:], start=True, stop=True)
                elif kind == "taps":
                    for i in range(2):
                        bank = take(("taps", i))
                        for k in range(2):
                            for c in range(C):
                                pe.wait_ge(diags_ready, c + 1)
                                last = pe.matmul(bank[:, k, c * P:(c + 1) * P], in_w_sb[:, c], taps_d[:, c, 2 * i + k],
                                                 start=True, stop=True)
                        last.then_inc(filled[BANK["taps", i][0]], 1)
                elif kind == "project":
                    pe.wait_ge(proj_loaded, 16 * 3)
                    bank = take(("project", 0))
                    W = DR + 2 * NS
                    for c in range(C):
                        last = pe.transpose(bank[:, c, 0:W], xproj_sb[:, c * P:(c + 1) * P], ident[0:W, 0:W])
                    last.then_inc(filled[BANK["project", 0][0]], 1)
                    bank = take(("project", 1))
                    for c in range(C):
                        last = pe.transpose(bank[0:DR, 0, c * P:(c + 1) * P], step_w_sb[:, c], ident[:])
                    last.then_inc(filled[BANK["project", 1][0]], 1)
                    bank = take(("project", 2))
                    pe.transpose(bank[:, 0, 0:GROUPS], a_log_sb[:], ident[0:GROUPS, 0:GROUPS]).then_inc(
                        filled[BANK["project", 2][0]], 1)
                elif kind == "context":
                    pe.wait_ge(ctx_loaded[b], 16)
                    if b == 0:
                        pe.wait_ge(masks_ready, 1)
                    bank = take(step)
                    for c in range(C):
                        last = pe.transpose(bank[:, 0, c * P:(c + 1) * P], ctx_sb[:, b, c], ident[:])
                    last.then_inc(filled[2], 1)
                elif kind == "conv":
                    q = step[2]
                    c = q // 2
                    if q == 0:
                        take(("conv", b))
                        pe.wait_ge(ctx_turned, b + 1)
                        pe.wait_ge(pads_ready, 1)
                        if b == 0:
                            pe.wait_ge(taps_ready, 2)
                    bank = work[BANK["conv", b][0]]
                    for k in range(2 * (q % 2), 2 * (q % 2) + 2):
                        last = pe.matmul(bank[:, c], in_taps[:, k, c * P:(c + 1) * P], ctx_t[:, b % 2, k:k + L],
                                         start=(k == 0), stop=(k == TAPS - 1))
                    if q == 3:
                        last.then_inc(filled[BANK["conv", b][0]], 1)
                elif kind == "x_dbl":
                    pe.wait_ge(u_ready, b + 1)
                    if b == 0:
                        pe.wait_ge(project_ready, 2)
                    bank = take(step)
                    for c in range(C):
                        last = pe.matmul(bank[0:2 * NS + DR, 0], xproj_t[:, c], u[:, b % 3, c], start=(c == 0), stop=(c == C - 1))
                    last.then_inc(filled[BANK[step][0]], 1)
                elif kind == "bc":
                    pe.wait_ge(bc_hi, b + 1)
                    pe.wait_ge(bc_lo, b + 1)
                    if b == 0:
                        pe.wait_ge(masks_cast, 2)
                    bank = take(step)
                    for i in range(2):
                        last = pe.matmul(bank[:, i], spread_bc[:, i], bc_parts[:], start=True, stop=True)
                    last.then_inc(filled[BANK[step][0]], 1)
                elif kind == "step":
                    pe.wait_ge(low_ready, b + 1)
                    bank = take(step)
                    for c in range(C):
                        last = pe.matmul(bank[:, c], step_wt[:, c * P:(c + 1) * P], low[:, b % 2], start=True, stop=True)
                    last.then_inc(filled[2], 1)
                elif kind == "ahead":
                    pe.wait_ge(masks_cast, 4)
                    for n in range(SPREAD_AHEAD):
                        spread_delta(n)
                        if n == 1:
                            spread_du(0)
                elif kind == "unit":
                    n = index(*step[1:])
                    if n + 1 < UNITS * B:
                        spread_du(n + 1)
                    if n + SPREAD_AHEAD < UNITS * B:
                        spread_delta(n + SPREAD_AHEAD)
                    if n % 2 == 0 and n >= 4:
                        sum_states(n // 2 - 2)
                elif kind == "flush":
                    for s in range(UNITS * B // 2 - 2, UNITS * B // 2):
                        sum_states(s)
                elif kind == "residual":
                    pe.wait_ge(mixed_ready, C * (b + 1))
                    bank = take(step)
                    for lt in range(C):
                        for c in range(C):
                            last = pe.transpose(bank[:, lt, c * P:(c + 1) * P], mixed[:, c, lt * P:(lt + 1) * P], ident[:])
                    last.then_inc(filled[BANK[step][0]], 1)
                elif kind == "normed":
                    pe.wait_ge(xn_ready, C * (b + 1))
                    bank = take(step)
                    for k in range(KB):
                        for lt in range(C):
                            last = pe.transpose(bank[:, k, lt * P:(lt + 1) * P], xn[:, lt, k * P:(k + 1) * P], ident[:])
                    last.then_inc(filled[BANK[step][0]], 1)
                elif kind in ("gate", "up"):
                    i, w = step[2], 0 if kind == "gate" else 1
                    if i == 0 and w == 0:
                        pe.wait_ge(xnt_hi_ready, b + 1)
                        pe.wait_ge(xnt_lo_ready, b + 1)
                        if b == 0:
                            pe.wait_ge(hi_ready, 4)
                            pe.wait_ge(lo_ready, 4)
                    bank = take(step)
                    for m in range(2):
                        j = 2 * (i % 2) + m
                        cols = slice((i // 2) * P, (i // 2 + 1) * P)
                        terms = [(a, x_, k) for k in range(KB) for a, x_ in ((up_hi, xnt_lo), (up_lo, xnt_hi), (up_hi, xnt_hi))]
                        for t, (a, x_, k) in enumerate(terms):
                            last = pe.matmul(bank[:, m], a[:, k, w, j, cols], x_[:, k], start=(t == 0),
                                             stop=(t == len(terms) - 1))
                    last.then_inc(filled[BANK[step][0]], 1)
                elif kind == "wins":
                    _, _, c, pair = step
                    pe.wait_ge(beats_ready, 3 * (2 * b + c + 1))
                    bank = take(step)
                    terms = (((plus_b, 0), (plus_b, 3), (plus_b, 5)), ((minus_b, 0), (plus_b, 1), (plus_b, 4)),
                             ((minus_b, 3), (minus_b, 1), (plus_b, 2)), ((minus_b, 5), (minus_b, 4), (minus_b, 2)))
                    for m in range(2):
                        for t, (sign, at) in enumerate(terms[2 * pair + m]):
                            last = pe.matmul(bank[:, m], sign[:], beats[:, c, at], start=(t == 0), stop=(t == 2))
                    last.then_inc(filled[BANK[step][0]], 1)
                elif kind == "down":
                    _, _, tt, c = step
                    one = b < B - 1
                    key = step[:2] if one else step[:3]
                    if c == 0 and not (one and tt):
                        take(key)
                        if b == 0:
                            pe.wait_ge(down_loaded, 16)
                    bank = work[BANK[key][0]]
                    for j in range(4):
                        pe.wait_ge(kept_ready, 8 * b + 4 * c + j + 1)
                        last = pe.matmul(bank[:, tt if one else 0], h_kept[:, c, j, tt * P:(tt + 1) * P], down_sb[:, c, j],
                                         start=(c == 0 and j == 0), stop=(c == IC - 1 and j == 3))
                    if c == IC - 1 and (tt or not one):
                        last.then_inc(filled[BANK[key][0]], 1)


_INS = ['x', 'ctx_1024', 'g_xattn', 'g_ffn', 'L0_xattn_in_proj_w', 'L0_xattn_conv_w', 'L0_xattn_conv_b',
        'L0_xattn_x_proj_w', 'L0_xattn_dt_proj_w', 'L0_xattn_dt_proj_b', 'L0_xattn_A_log', 'L0_xattn_D',
        'L0_ffn_w_gate', 'L0_ffn_w_up', 'L0_ffn_w_down']


def kernel(**inputs):
    import numpy as _np
    import concourse.bacc as _bacc
    from concourse.bass_utils import run_bass_kernel_spmd as _run

    nc = _bacc.Bacc("TRN2", target_bir_lowering=False, num_devices=1)
    arrays, args = {}, []
    for name in _INS:
        a = _np.ascontiguousarray(inputs[name])
        arrays[f"in_{name}_dram"] = a
        args.append(nc.dram_tensor(f"in_{name}_dram", a.shape, mybir.dt.from_np(a.dtype), kind="ExternalInput").ap())
    args.append(nc.dram_tensor("out_dram", (B, L, D_IN), mybir.dt.float32, kind="ExternalOutput").ap())
    gated_block(nc, *args)
    r = _run(nc, [arrays], core_ids=[0])
    return r.results[0]["out_dram"]
```

```python
from contextlib import ExitStack

import concourse.bass as bass
from concourse import mybir

B, L, D_CTX, D_IN, NS, DR, TAPS, HID = 4, 256, 128, 256, 16, 8, 4, 1024
P = 128
C = D_IN // P
ES = P // NS
GROUPS = D_IN // ES
UNITS = GROUPS // 2
QUADS = 4
SETS = GROUPS // C // QUADS
KB = D_IN // P
IC = HID // (4 * P)
EPS = 1e-5

N_DECAY = 6
N_DRIVE = 3
N_STATE = 4
N_PROD = 6
WORK = 3
WARM = 40
SPREAD_AHEAD = 4


T, A, V, G, S = "tensor", "scalar", "vector", "gpsimd", "sync"
ALL = (T, A, V, G, S)


FRONT_1 = {
    ("step",): dict(T=5), ("gate_in",): dict(A=1), ("x_dbl",): dict(T=3, V=4), ("softplus",): dict(A=7, V=7, G=7),
    ("delta",): dict(G=7), ("bc",): dict(T=9, A=10), ("shift",): dict(V=2), ("halves", 0): dict(A=9, V=11),
    ("halves", 1): dict(A=10, V=11, S=11), ("context",): dict(V=0, G=0),
}
FRONT_2 = {
    ("context",): dict(T=-5, A=-5, V=-4, G=-3), ("conv", 1): dict(T=-3), ("shift",): dict(V=2),
    ("conv", 2): dict(T=-3), ("conv", 3): dict(T=-1), ("delta",): dict(G=7), ("gate_in",): dict(A=-1),
    ("x_dbl",): dict(T=3, V=5), ("conv", 0): dict(T=-5), ("step",): dict(T=6), ("halves", 1): dict(A=10, V=11, S=11),
    ("halves", 0): dict(A=10, V=11), ("softplus",): dict(A=6, V=7, G=6), ("bc",): dict(T=8, A=9),
}
FRONT_3 = {
    ("context",): dict(T=-6, A=-5, V=-2, G=-4), ("shift",): dict(V=1), ("conv", 0): dict(T=-3),
    ("conv", 1): dict(T=-1), ("conv", 2): dict(T=-1), ("gate_in",): dict(A=1), ("conv", 3): dict(T=-1),
    ("step",): dict(T=5), ("x_dbl",): dict(T=3, V=4), ("delta",): dict(G=7), ("halves", 1): dict(A=10, V=11, S=11),
    ("softplus",): dict(A=5, V=8, G=6), ("bc",): dict(T=10, A=10), ("halves", 0): dict(A=9, V=10),
}
EARLY = {
    ("shift",): dict(V=1), ("split_up", 2): dict(A=13, G=13), ("split_up", 0): dict(A=1, G=5),
    ("context",): dict(V=0, G=0), ("split_up", 3): dict(A=13, V=14), ("split_up", 1): dict(A=3, V=5),
}
BEHIND = {
    ("finish", 0): dict(V=12, G=12), ("finish", 1): dict(V=18, G=18), ("residual",): dict(T=21, V=21, G=21),
    ("norm",): dict(V=22), ("normed",): dict(T=23, A=23, V=24), ("gate", 1): dict(T=26, A=26),
    ("up", 0): dict(T=30, V=30), ("gate", 2): dict(T=27, A=27), ("gate", 0): dict(T=25, A=25),
    ("gate", 3): dict(T=27, A=28), ("silu",): dict(A=28), ("up", 1): dict(T=31, V=31), ("up", 3): dict(T=32, V=33),
    ("wins", 0, 0): dict(T=34, V=34), ("up", 2): dict(T=31, V=32), ("wins", 1, 1): dict(T=37, V=37),
    ("compare", 0): dict(A=32, V=33), ("wins", 0, 1): dict(T=34, V=34), ("compare", 1): dict(A=34, V=35),
    ("down", 0, 0): dict(T=38), ("down", 0, 1): dict(T=38), ("result", None): dict(V=41, S=39),
    ("down", 1, 0): dict(T=40), ("wins", 1, 0): dict(T=36, V=36), ("down", 1, 1): dict(T=41),
}
BEHIND_1 = {
    ("finish", 0): dict(V=10, G=14), ("norm",): dict(V=22), ("residual",): dict(T=21, V=21, G=21),
    ("finish", 1): dict(V=18, G=17), ("normed",): dict(T=23, A=23, V=24), ("gate", 0): dict(T=25, A=25),
    ("gate", 1): dict(T=25, A=26), ("gate", 2): dict(T=26, A=27), ("gate", 3): dict(T=27, A=29),
    ("silu",): dict(A=29), ("compare", 0): dict(A=32, V=34), ("up", 1): dict(T=30, V=31), ("up", 0): dict(T=29, V=30),
    ("up", 3): dict(T=33, V=34), ("wins", 0, 1): dict(T=36, V=37), ("wins", 0, 0): dict(T=34, V=35),
    ("up", 2): dict(T=31, V=32), ("compare", 1): dict(A=35, V=36), ("wins", 1, 0): dict(T=37, V=37),
    ("down", 0, 0): dict(T=38), ("down", 0, 1): dict(T=38), ("down", 1, 0): dict(T=38), ("down", 1, 1): dict(T=40),
    ("result", None): dict(V=41, S=41), ("wins", 1, 1): dict(T=37, V=37),
}
BEHIND_2 = {
    ("finish", 0): dict(V=10, G=12), ("finish", 1): dict(V=19, G=18), ("residual",): dict(T=21, V=21, G=21),
    ("norm",): dict(V=21), ("normed",): dict(T=23, A=23, V=24), ("gate", 0): dict(T=25, A=26),
    ("gate", 1): dict(T=26, A=26), ("gate", 2): dict(T=27, A=27), ("gate", 3): dict(T=27, A=30),
    ("up", 0): dict(T=29, V=30), ("up", 1): dict(T=30, V=31), ("up", 2): dict(T=30, V=31), ("silu",): dict(A=31),
    ("up", 3): dict(T=30, V=31), ("compare", 0): dict(A=31),
}
TAIL = [
    ("V", ("compare", 2, 0)), ("V", ("finish", 3, 1)), ("T", ("flush",)), ("T", ("wins", 2, 0, 0)),
    ("G", ("finish", 3, 1)), ("T", ("wins", 2, 0, 1)), ("A", ("compare", 2, 1)), ("V", ("wins", 2, 0, 0)),
    ("V", ("wins", 2, 0, 1)), ("TVG", ("residual", 3)), ("T", ("down", 2, 1, 0)), ("AV", ("norm", 3)),
    ("V", ("compare", 2, 1)), ("TAV", ("normed", 3)), ("T", ("down", 2, 0, 0)), ("T", ("wins", 2, 1, 0)),
    ("T", ("wins", 2, 1, 1)), ("V", ("wins", 2, 1, 0)), ("T", ("up", 3, 1)), ("T", ("gate", 3, 0)),
    ("A", ("gate", 3, 0)), ("TA", ("gate", 3, 1)), ("V", ("wins", 2, 1, 1)), ("V", ("up", 3, 1)),
    ("S", ("result", 2, 0)), ("A", ("compare", 3, 0)), ("TV", ("up", 3, 0)), ("T", ("down", 2, 0, 1)),
    ("T", ("down", 2, 1, 1)), ("V", ("result", 2, 0)), ("V", ("compare", 3, 0)), ("S", ("result", 2, 1)),
    ("A", ("gate", 3, 2)), ("T", ("gate", 3, 2)), ("TA", ("gate", 3, 3)), ("V", ("wins", 3, 0, 0)),
    ("T", ("wins", 3, 0, 0)), ("V", ("result", 2, 1)), ("A", ("compare", 3, 1)), ("T", ("up", 3, 2)),
    ("V", ("up", 3, 2)), ("TV", ("up", 3, 3)), ("TV", ("wins", 3, 0, 1)), ("T", ("down", 3, 0, 0)),
    ("V", ("compare", 3, 1)), ("V", ("wins", 3, 1, 0)), ("T", ("down", 3, 1, 0)), ("T", ("wins", 3, 1, 0)),
    ("TV", ("wins", 3, 1, 1)), ("VS", ("result", 3, 0)), ("T", ("down", 3, 0, 1)), ("T", ("down", 3, 1, 1)),
    ("V", ("result", 3, 1)), ("S", ("result", 3, 1)),
]
HOLD = {1: 1, 2: 1, 3: 2, 4: 1}
ENGINES = {"T": "tensor", "A": "scalar", "V": "vector", "G": "gpsimd", "S": "sync"}


def order():
    steps = [((T, A), ("load",)), ((G,), ("masks",)), ((T, A), ("context", 0)), (ALL, ("taps",)), ((A,), ("masks",))]
    steps += [((T,), ("conv", 0, q)) for q in range(4)]
    steps += [((T, V), ("project",)), ((A,), ("gate_in", 0)), ((T, V), ("x_dbl", 0)), ((T, A), ("step", 0)),
              ((T,), ("bc", 0)), ((T, A), ("context", 1)), *(((T,), ("conv", 1, q)) for q in range(4)),
              ((A, V), ("softplus", 0)), ((A,), ("project",)), ((A,), ("tables",)), ((A,), ("bc", 0)),
              (ALL, ("delta", 0)), ((A, V, G), ("halves", 0)), (ALL, ("ahead",))]
    at = {n: [] for n in range(B * UNITS)}
    last = {("finish", 0): BEHIND["finish", 0]}
    for b, start, table in ((0, 0, EARLY), (1, 0, FRONT_1), (2, UNITS, FRONT_2), (3, 2 * UNITS, FRONT_3), (0, 0, BEHIND),
                            (1, UNITS, BEHIND_1), (2, 2 * UNITS, BEHIND_2), (3, 3 * UNITS, last)):
        for key, slots in table.items():
            for engine, slot in slots.items():
                step = key if key[0] == "split_up" else (key[0], b) + key[1:]
                at[start + slot].append(((ENGINES[engine],), step))
    for n in range(B * UNITS):
        steps.append((ALL, ("unit", n // UNITS, n % UNITS)))
        steps += at[n]
    steps += [(tuple(ENGINES[e] for e in engines), step) for engines, step in TAIL]
    return steps


def table_windows(steps):
    unit, found = None, []
    for engines, s in steps:
        if s[0] == "unit":
            unit = UNITS * s[1] + s[2]
        elif s[0] in ("gate_in", "silu") and unit is not None:
            found.append(unit)
    return found


def spread_by(n, windows):
    late = max(HOLD.get(n - w, 0) for w in windows)
    return min(n + SPREAD_AHEAD - late, B * UNITS - 1)


def banks(steps):
    used, at = [[] for _ in range(WORK + 5)], {}
    for engines, s in steps:
        kind = s[0]
        if T not in engines:
            continue
        if kind in ("x_dbl", "bc") and s[1] == 0:
            keys, bank = [s], 1
        elif s[:2] in (("context", 1), ("conv", 1)) and s[2:] in ((), (0,)):
            keys, bank = [s[:2]], WORK if kind == "context" else WORK + 4
        elif kind in ("context", "x_dbl", "step", "bc") or (kind == "conv" and s[2] == 0):
            keys, bank = [s[:2] if kind == "conv" else s], 2
        elif kind == "project":
            keys, bank = [("project", i) for i in range(3)], 0
        elif kind in ("residual", "normed"):
            keys, bank = [s], 0
        elif kind in ("gate", "up"):
            keys, bank = [s], s[2] % 2 + (2 if kind == "up" and s[1] == B - 1 else 0)
        elif kind == "wins":
            keys, bank = [s], s[3]
        elif kind == "taps":
            keys, bank = [("taps", 0)], 0
        elif kind == "down" and s[1] >= B - 2 and s[3] == 0:
            keys, bank = [s[:3]], (4 if s[1] == B - 1 else 6) + s[2]
        elif kind == "down" and s[1] < B - 2 and s[2:] == (0, 0):
            keys, bank = [s[:2]], 1
        else:
            continue
        for i, key in enumerate(keys):
            n = bank + i % 2 if kind in ("taps", "project") else bank
            at[key] = (n, len(used[n]), used[n][-1] if used[n] else None)
            used[n].append(key)
    return at


def group(k, half):
    within = k % (UNITS // C)
    quad = 2 * (within % 2) + half
    return quad * SETS + within // 2, quad


def gated_block(nc, x, ctx_in, g_mix, g_ffn, in_w, conv_w, conv_b, xproj_w, step_w, step_b, a_log, skip,
                w_gate, w_up, w_down, out):
    F32, BF16, F32R = mybir.dt.float32, mybir.dt.bfloat16, mybir.dt.float32r
    ALU, ACT = mybir.AluOpType, mybir.ActivationFunctionType
    STEPS = order()
    BANK = banks(STEPS)
    WINDOWS = table_windows(STEPS)

    with ExitStack() as stack:
        def sb(name, shape, dt=F32):
            return stack.enter_context(nc.sbuf_tensor(name, shape, dt))

        def sem(name):
            return stack.enter_context(nc.semaphore(name))

        x_sb = sb("x_sb", [P, B, C, L])
        ctx_sb = sb("ctx_sb", [P, B, C, D_CTX])
        in_w_sb = sb("in_w_sb", [P, C, D_CTX])
        conv_b_sb = sb("conv_b_sb", [P, C])
        step_b_sb = sb("step_b_sb", [P, C])
        skip_sb = sb("skip_sb", [P, C])
        xproj_sb = sb("xproj_sb", [DR + 2 * NS, D_IN])
        step_w_sb = sb("step_w_sb", [P, C, DR])
        a_log_sb = sb("a_log_sb", [GROUPS, P])
        gains_sb = sb("gains_sb", [P, 2])
        up_raw = sb("up_raw", [P, KB, 2, HID])
        down_sb = sb("down_sb", [P, IC, 4, D_IN])
        ident = sb("ident", [P, P])
        plus_b = sb("plus_b", [P, P], BF16)
        minus_b = sb("minus_b", [P, P], BF16)
        spread_r = sb("spread_r", [P, ES, P], F32R)
        spread_bc_f = sb("spread_bc_f", [4 * NS, 2, P])
        spread_bc = sb("spread_bc", [4 * NS, 2, P], F32R)
        warm = sb("warm", [P, P], BF16)
        gather = sb("gather", [P, SETS, 32])
        power = sb("power", [P, C])
        in_taps = sb("in_taps", [P, TAPS, D_IN])
        xproj_t = sb("xproj_t", [P, C, DR + 2 * NS])
        step_wt = sb("step_wt", [DR, D_IN])
        a_exp = sb("a_exp", [P, GROUPS])
        a_neg = sb("a_neg", [P, GROUPS])
        gains = sb("gains", [P, 2])
        up_hi = sb("up_hi", [P, KB, 2, 4, D_IN], F32R)
        up_lo = sb("up_lo", [P, KB, 2, 4, D_IN], F32R)
        ctx_t = sb("ctx_t", [P, 2, TAPS - 1 + L])
        stats = sb("stats", [P, B, C, 6])
        moments = sb("moments", [P, B, C, 2])
        veps = sb("veps", [P, B, C])
        rstd = sb("rstd", [P, B, C])
        shift = sb("shift", [P, B, C])
        z_gate = sb("z_gate", [P, 2, C, L])
        u = sb("u", [P, 3, C, L])
        bc_parts = sb("bc_parts", [4 * NS, L], F32R)
        bc = sb("bc", [P, 2, 2, L])
        low = sb("low", [DR, 2, L])
        sp_abs = sb("sp_abs", [P, C, L])
        sp_exp = sb("sp_exp", [P, C, L])
        sp_pos = sb("sp_pos", [P, C, L])
        sp_ln = sb("sp_ln", [P, C, L])
        sp_back = sb("sp_back", [P, C, L])
        sp_lost = sb("sp_lost", [P, C, L])
        du_parts = sb("du_parts", [P, 2, C, L], F32R)
        delta = sb("delta", [P, C, L])
        du = sb("du", [P, C, L])
        delta_h = sb("delta_h", [P, 2, 2, C, L], F32R)
        du_h = sb("du_h", [P, 2, 2, C, L], F32R)
        decay = sb("decay", [P, N_DECAY, 2, L])
        drive = sb("drive", [P, N_DRIVE, 2, L])
        state = sb("state", [P, N_STATE, 2, L])
        prod = sb("prod", [P, N_PROD, 2, L])
        mixed = sb("mixed", [P, C, L])
        x2 = x_sb
        stats2 = sb("stats2", [P, B, C, 6])
        moments2 = sb("moments2", [P, B, C, 2])
        veps2 = sb("veps2", [P, B, C])
        rstd2 = sb("rstd2", [P, B, C])
        xn = sb("xn", [P, C, L])
        xnt_hi = sb("xnt_hi", [P, KB, L], F32R)
        xnt_lo = sb("xnt_lo", [P, KB, L], F32R)
        gate_s = up_raw[:, 0].rearrange("p w (j t) -> p w j t", j=4)
        h = sb("h", [P, IC, 4, L])
        tap_rows = h[:, 0]
        spread_f = h[:, 1].rearrange("p j (k q) -> p (j k) q", q=P)
        h_abs = up_raw[:, 1].rearrange("p w (j t) -> p w j t", j=4)
        beats = sb("beats", [P, IC, 6, L], BF16)
        h_kept = sb("h_kept", [P, IC, 4, L])

        dec_ps = [stack.enter_context(nc.psum_tensor(f"dec_ps{i}", [P, 2, L], F32)) for i in range(2)]
        drv_ps = [stack.enter_context(nc.psum_tensor(f"drv_ps{i}", [P, 2, L], F32)) for i in range(2)]
        y_ps = stack.enter_context(nc.psum_tensor("y_ps", [P, C, L], F32))
        work = [stack.enter_context(nc.psum_tensor(f"work{i}", [P, 2, L], F32)) for i in range(WORK)]
        work += drv_ps + dec_ps + [y_ps]

        ctx_loaded = [sem(f"ctx_loaded{b}") for b in range(B)]
        x_loaded = [sem(f"x_loaded{b}") for b in range(B)]
        taps_loaded, proj_loaded, small_loaded = sem("taps_loaded"), sem("proj_loaded"), sem("small_loaded")
        up_loaded, down_loaded = sem("up_loaded"), sem("down_loaded")
        stored = [sem(f"stored{b}") for b in range(B)]
        warm_ready, blank, masks_ready, pads_ready = sem("warm_ready"), sem("blank"), sem("masks_ready"), sem("pads_ready")
        masks_cast, taps_ready = sem("masks_cast"), sem("taps_ready")
        project_ready, a_raw, a_ready, gains_ready = sem("project_ready"), sem("a_raw"), sem("a_ready"), sem("gains_ready")
        hi_ready, lo_ready = sem("hi_ready"), sem("lo_ready")
        filled = [sem(f"filled{i}") for i in range(WORK + 5)]
        ctx_turned = sem("ctx_turned")
        x_stats, x_moments, x_veps, x_rstd, x_shift = (sem(n) for n in ("x_stats", "x_moments", "x_veps", "x_rstd", "x_shift"))
        u_ready, z_ready, bc_hi, bc_lo, bc_ready, low_ready = (
            sem(n) for n in ("u_ready", "z_ready", "bc_hi", "bc_lo", "bc_ready", "low_ready"))
        abs_ready, pos_ready, exp_ready, ln_ready = (sem(n) for n in ("abs_ready", "pos_ready", "exp_ready", "ln_ready"))
        back_ready, lost_ready, sum_ready, delta_ready, du_ready = (
            sem(n) for n in ("back_ready", "lost_ready", "sum_ready", "delta_ready", "du_ready"))
        delta_hi, delta_lo, du_hi, du_lo = (sem(n) for n in ("delta_hi", "delta_lo", "du_hi", "du_lo"))
        delta_lo_1, du_moved = sem("delta_lo_1"), sem("du_moved")
        zero_col = sem("zero_col")
        delta_spread, du_spread, decay_ready, drive_ready, scanned, prod_ready, summed = (
            sem(n) for n in ("delta_spread", "du_spread", "decay_ready", "drive_ready", "scanned", "prod_ready", "summed"))
        skip_added, mixed_ready, x2_ready = sem("skip_added"), sem("mixed_ready"), sem("x2_ready")
        s_stats, s_moments, s_veps, s_rstd, xn_ready = (sem(n) for n in ("s_stats", "s_moments", "s_veps", "s_rstd", "xn_ready"))
        xnt_hi_ready, xnt_lo_ready, gate_out, gate_ready, h_ready, h_abs_ready = (
            sem(n) for n in ("xnt_hi_ready", "xnt_lo_ready", "gate_out", "gate_ready", "h_ready", "h_abs_ready"))
        beats_ready, kept_ready, result_ready = (
            sem(n) for n in ("beats_ready", "kept_ready", "result_ready"))

        block = stack.enter_context(nc.Block())

        def steps_of(engine):
            return [step for engines, step in STEPS if engine in engines]

        def has(eng, key):
            n, before, _ = BANK[key]
            eng.wait_ge(filled[n], before + 1)
            return work[n]

        def last_read(key):
            kind, b = key[0], key[1]
            if kind == "wins":
                return kept_ready, 8 * b + 4 * key[2] + 2 * key[3] + 2
            return {
                "taps": lambda: (taps_ready, TAPS), "project": lambda: (project_ready, b + 1),
                "context": lambda: (ctx_turned, b + 1), "conv": lambda: (u_ready, b + 1),
                "bc": lambda: (bc_ready, b + 1), "x_dbl": lambda: (bc_lo, b + 1),
                "step": lambda: (pos_ready, b + 1), "residual": lambda: (x2_ready, C * (b + 1)),
                "normed": lambda: (xnt_lo_ready, b + 1),
                "gate": lambda: (gate_ready if b == B - 1 else gate_out, 4 * b + key[2] + 1),
                "up": lambda: (h_ready, 4 * b + key[2] + 1),
                "down": lambda: (result_ready, C * (b + 1) if len(key) == 2 else C * b + key[2] + 1),
            }[kind]()

        def direct(b, which):
            return which == 0 or b == 0

        def index(b, k):
            return UNITS * b + k

        def lower_half(eng, src, dst, parity, q, hi, count, done):
            eng.wait_ge(hi, count)
            rows, other = slice(64 * q, 64 * q + 64), slice(64 - 64 * q, 128 - 64 * q)
            eng.tensor_tensor(dst[other, parity, q], src[rows], dst[rows, parity, q].bitcast(F32),
                              ALU.subtract).then_inc(done, 1)

        @block.sync
        def _(sp):
            sp.dma_start(in_w_sb[:], in_w.rearrange("(c p) d -> p c d", p=P)).then_inc(taps_loaded, 16)
            sp.dma_start(tap_rows.rearrange("p j t -> p (j t)"),
                         conv_w.rearrange("e k -> (e k)")[None, :].broadcast_to([P, D_IN * TAPS])).then_inc(taps_loaded, 16)
            sp.dma_start(ctx_sb[:, 0], ctx_in[0].rearrange("(c p) d -> p c d", p=P)).then_inc(ctx_loaded[0], 16)
            sp.dma_start(xproj_sb[:], xproj_w).then_inc(proj_loaded, 16)
            sp.dma_start(step_w_sb[:], step_w.rearrange("(c p) r -> p c r", p=P)).then_inc(proj_loaded, 16)
            sp.dma_start(a_log_sb[:], a_log.rearrange("(g e) n -> g (e n)", e=ES)).then_inc(proj_loaded, 16)
            for dst, src in ((conv_b_sb, conv_b), (step_b_sb, step_b), (skip_sb, skip)):
                sp.dma_start(dst[:], src.rearrange("(c p) -> p c", p=P), allow_slow_non_contiguous=True).then_inc(small_loaded, 16)
            sp.dma_start(gains_sb[:, 0:1], g_mix[None, :].broadcast_to([P, 1])).then_inc(small_loaded, 16)
            sp.dma_start(gains_sb[:, 1:2], g_ffn[None, :].broadcast_to([P, 1])).then_inc(small_loaded, 16)
            sp.dma_start(ctx_sb[:, 1], ctx_in[1].rearrange("(c p) d -> p c d", p=P)).then_inc(ctx_loaded[1], 16)
            sp.dma_start(x_sb[:, 0], x[0].rearrange("(c p) d -> p c d", p=P)).then_inc(x_loaded[0], 16)
            for b in range(1, B):
                if b > 1:
                    sp.dma_start(ctx_sb[:, b], ctx_in[b].rearrange("(c p) d -> p c d", p=P)).then_inc(ctx_loaded[b], 16)
                sp.dma_start(x_sb[:, b], x[b].rearrange("(c p) d -> p c d", p=P)).then_inc(x_loaded[b], 16)
            sp.dma_start(up_raw[:, :, 0], w_gate.rearrange("(k p) i -> p k i", p=P)).then_inc(up_loaded, 16)
            sp.dma_start(up_raw[:, :, 1], w_up.rearrange("(k p) i -> p k i", p=P)).then_inc(up_loaded, 16)
            sp.dma_start(down_sb[:], w_down.rearrange("(c p j) n -> p c j n", p=P, j=4)).then_inc(down_loaded, 16)
            for step in steps_of(S):
                if step[0] == "halves":
                    b = step[1]
                    if b >= 2:
                        sp.wait_ge(du_spread, UNITS * (b - 1))
                    for part, ready in ((0, du_hi), (1, du_lo)):
                        sp.wait_ge(ready, b + 2)
                        for q in range(2):
                            to = 64 * (q ^ part)
                            sp.dma_start(du_h[to:to + 64, b % 2, q].bitcast(F32),
                                         du_parts[64 * q:64 * q + 64, part].bitcast(F32)).then_inc(du_moved, 16)
                elif step[0] == "result":
                    _, b, tt = step
                    if tt is None:
                        sp.wait_ge(result_ready, C * (b + 1))
                        sp.dma_start(out[b].rearrange("(c p) d -> p c d", p=P), x2[:, b]).then_inc(stored[b], 16)
                    else:
                        sp.wait_ge(result_ready, C * b + tt + 1)
                        sp.dma_start(out[b, tt * P:(tt + 1) * P], x2[:, b, tt]).then_inc(stored[b], 16)
            for b in range(B):
                sp.wait_ge(stored[b], 16 if b < B - 2 else 32)

        @block.gpsimd
        def _(pool):
            for step in steps_of(G):
                kind, b = step[0], step[1] if len(step) > 1 else None
                if kind == "masks":
                    pool.memset(warm[:], 0.0).then_inc(warm_ready, 1)
                    pool.memset(ident[:], 0.0).then_inc(blank, 1)
                    pool.memset(ctx_t[:, :, 0:TAPS - 1], 0.0).then_inc(pads_ready, 1)
                    pool.memset(spread_f[:], 0.0).then_inc(blank, 1)
                    pool.memset(spread_bc_f[:], 0.0).then_inc(blank, 1)
                    pool.memset(gather[:], 1.0).then_inc(blank, 1)
                    pool.memset(power[:], -0.5).then_inc(pads_ready, 1)
                    pool.memset(decay[:, :, :, 0:1], 0.0).then_inc(zero_col, 1)
                    pool.wait_ge(blank, 4)
                    pool.affine_select(out=ident[:], in_=ident[:], compare_op=ALU.not_equal, fill=1.0, base=0,
                                       pattern=[[-1, P]], channel_multiplier=1).then_inc(masks_ready, 1)
                    wide = spread_f[:].rearrange("p g (e n) -> p g e n", n=NS)
                    for rows, base in ((0, 0), (1, -64)):
                        pool.affine_select(out=wide, in_=wide, compare_op=ALU.not_equal, fill=1.0, base=base,
                                           pattern=[[-ES, ES], [-1, ES], [0, NS]],
                                           channel_multiplier=1).then_inc(masks_ready, 1)
                        pool.wait_ge(masks_ready, 2 + rows)
                    wide = spread_bc_f[:].rearrange("p i (e n) -> p i e n", n=NS)
                    for rows, base in ((0, 0), (1, -2 * NS)):
                        pool.affine_select(out=wide, in_=wide, compare_op=ALU.not_equal, fill=1.0, base=base,
                                           pattern=[[-NS, 2], [0, ES], [-1, NS]],
                                           channel_multiplier=1).then_inc(masks_ready, 1)
                        pool.wait_ge(masks_ready, 4 + rows)
                    pool.affine_select(out=gather[:], in_=gather[:], compare_op=ALU.is_ge, fill=0.0, base=0,
                                       pattern=[[P, SETS], [-NS, 32]], channel_multiplier=1).then_inc(masks_ready, 1)
                    pool.wait_ge(masks_ready, 6)
                    pool.affine_select(out=gather[:], in_=gather[:], compare_op=ALU.is_ge, fill=0.0, base=NS - 1,
                                       pattern=[[-P, SETS], [NS, 32]], channel_multiplier=-1).then_inc(masks_ready, 1)
                elif kind == "context":
                    pool.wait_ge(pads_ready, 2)
                    pool.wait_ge(x_veps, b + 1)
                    pool.tensor_tensor(rstd[:, b], veps[:, b], power[:], ALU.pow).then_inc(x_rstd, 1)
                elif kind == "split_up":
                    k, w = divmod(step[1], 2)
                    if step[1] % 2:
                        continue
                    pool.wait_ge(hi_ready, step[1] + 1)
                    pool.tensor_tensor(up_lo[:, k, w], up_raw[:, k, w].rearrange("p (g j) -> p j g", j=4),
                                       up_hi[:, k, w].bitcast(F32), ALU.subtract).then_inc(lo_ready, 1)
                elif kind == "softplus":
                    pool.wait_ge(pos_ready, b + 1)
                    pool.wait_ge(lost_ready, b + 1)
                    pool.tensor_tensor(sp_abs[:], sp_pos[:], sp_lost[:], ALU.add).then_inc(sum_ready, 1)
                elif kind == "delta" and b:
                    pool.wait_ge(ln_ready, b + 1)
                    pool.wait_ge(sum_ready, b + 1)
                    pool.wait_ge(delta_hi, 2 * b)
                    pool.wait_ge(delta_lo, 2 * b - 1)
                    pool.tensor_tensor(delta[:], sp_abs[:], sp_ln[:], ALU.add).then_inc(delta_ready, 1)
                    pool.wait_ge(delta_ready, b + 1)
                    pool.wait_ge(du_hi, b + 1)
                    pool.wait_ge(du_lo, b + 1)
                    pool.tensor_tensor(du[:], delta[:], u[:, b % 3], ALU.mult).then_inc(du_ready, 1)
                elif kind == "halves":
                    lower_half(pool, delta, delta_h, 0, 1, delta_hi, 2, delta_lo_1)
                    pool.wait_ge(delta_lo_1, 1)
                elif kind == "unit":
                    n = index(*step[1:])
                    pool.wait_ge(scanned, n + 1)
                    pool.wait_ge(bc_ready, b + 1)
                    if n >= N_PROD:
                        pool.wait_ge(summed, (n - N_PROD) // 2 + 1)
                    pool.tensor_tensor(prod[:, n % N_PROD], state[:, n % N_STATE],
                                       bc[:, b % 2, 1:2].broadcast_to([P, 2, L]), ALU.mult).then_inc(prod_ready, 1)
                elif kind == "finish":
                    n = C * b + step[2]
                    pool.wait_ge(skip_added, n + 1)
                    pool.wait_ge(z_ready, b + 1)
                    pool.tensor_tensor(mixed[:, step[2]], mixed[:, step[2]], z_gate[:, b % 2, step[2]],
                                       ALU.mult).then_inc(mixed_ready, 1)
                elif kind == "residual":
                    pool.wait_ge(s_veps, b + 1)
                    pool.tensor_tensor(rstd2[:, b], veps2[:, b], power[:], ALU.pow).then_inc(s_rstd, 1)

        @block.scalar
        def _(act):
            def z_gate_of(z):
                act.wait_ge(x_shift, z + 1)
                for c in range(C):
                    last = act.activation(z_gate[:, z % 2, c], x_sb[:, z, c], ACT.Silu,
                                          bias=shift[:, z, c:c + 1], scale=rstd[:, z, c:c + 1])
                last.then_inc(z_ready, 1)

            def decay_of(n):
                b, k = divmod(n, UNITS)
                act.wait_ge(delta_spread, n + 1)
                if n == 0:
                    act.wait_ge(zero_col, 1)
                if n >= N_DECAY:
                    act.wait_ge(scanned, n - N_DECAY + 1)
                for half in range(2):
                    g, _ = group(k, half)
                    col = (k // (UNITS // C)) * (GROUPS // C) + g
                    last = act.activation(decay[:, n % N_DECAY, half, 1:L], dec_ps[n % 2][:, half, 1:L], ACT.Exp,
                                          scale=a_neg[:, col:col + 1])
                last.then_inc(decay_ready, 1)

            for step in steps_of(A):
                kind, b = step[0], step[1] if len(step) > 1 else None
                if kind == "load":
                    act.preload_act_table_set("silu_and_others")
                elif kind == "masks":
                    act.wait_ge(masks_ready, 7)
                    act.activation(spread_r[:], spread_f[:], ACT.Copy).then_inc(masks_cast, 1)
                    act.activation(spread_bc[:], spread_bc_f[:], ACT.Copy).then_inc(masks_cast, 1)
                    act.activation(plus_b[:], ident[:], ACT.Copy).then_inc(masks_cast, 1)
                    act.activation(minus_b[:], ident[:], ACT.Copy, scale=-1.0).then_inc(masks_cast, 1)
                elif kind == "project":
                    act.wait_ge(project_ready, 2)
                    bank = has(act, ("project", 2))
                    act.activation(a_exp[:], bank[:, 0, 0:GROUPS], ACT.Copy).then_inc(project_ready, 1)
                elif kind == "context":
                    bank = has(act, step)
                    if b:
                        act.wait_ge(pads_ready, 1)
                    if b >= 2:
                        has(act, ("conv", b - 2))
                    act.activation(ctx_t[:, b % 2, TAPS - 1:], bank[:].rearrange("p a t -> p (a t)")[:, 0:L],
                                   ACT.Copy).then_inc(ctx_turned, 1)
                elif kind == "gate_in":
                    if b:
                        act.preload_act_table_set("silu_and_others")
                    else:
                        act.wait_ge(small_loaded, 16 * 5)
                        act.activation(gains[:], gains_sb[:], ACT.Tanh).then_inc(gains_ready, 1)
                    bank = has(act, ("conv", b))
                    if b >= 3:
                        act.wait_ge(mixed_ready, C * (b - 2))
                    for c in range(C):
                        last = act.activation(u[:, b % 3, c], bank[:, c], ACT.Silu, bias=conv_b_sb[:, c:c + 1])
                    last.then_inc(u_ready, 1)
                    if b == 1:
                        z_gate_of(0)
                        z_gate_of(1)
                    act.preload_act_table_set("natural_log_exp_and_others")
                elif kind == "bc":
                    bank = has(act, step)
                    if b >= 2:
                        act.wait_ge(scanned, UNITS * (b - 1))
                        act.wait_ge(prod_ready, UNITS * (b - 1))
                    act.activation(bc[:, b % 2], bank[:], ACT.Copy).then_inc(bc_ready, 1)
                elif kind == "softplus":
                    bank = has(act, ("step", b))
                    if b:
                        act.wait_ge(exp_ready, b)
                        act.wait_ge(lost_ready, b)
                        act.wait_ge(sum_ready, b)
                        act.wait_ge(delta_ready, b)
                    for c in range(C):
                        last = act.activation(sp_abs[:, c], bank[:, c], ACT.Abs, bias=step_b_sb[:, c:c + 1])
                    last.then_inc(abs_ready, 1)
                    act.wait_ge(abs_ready, b + 1)
                    act.activation(sp_exp[:], sp_abs[:], ACT.Exp, scale=-1.0).then_inc(exp_ready, 1)
                    act.wait_ge(exp_ready, b + 1)
                    act.activation(sp_ln[:], sp_exp[:], ACT.Ln, bias=1.0).then_inc(ln_ready, 1)
                    if b:
                        for c in range(C):
                            last = act.activation(sp_pos[:, c], bank[:, c], ACT.Relu, bias=step_b_sb[:, c:c + 1])
                        last.then_inc(pos_ready, 1)
                elif kind == "halves":
                    if b == 0:
                        for src, dst, ready, done, q in ((delta, delta_h, delta_ready, delta_hi, 0), (delta, delta_h, delta_ready, delta_hi, 1),
                                                         (du, du_h, du_ready, du_hi, 0), (du, du_h, du_ready, du_hi, 1)):
                            rows = slice(64 * q, 64 * q + 64)
                            act.wait_ge(ready, 1)
                            act.activation(dst[rows, 0, q], src[rows], ACT.Copy).then_inc(done, 1)
                        continue
                    src, ready, done = ((delta, delta_ready, delta_hi), (du, du_ready, du_hi))[step[2]]
                    act.wait_ge(ready, b + 1)
                    if direct(*step[1:]):
                        if b >= 2:
                            act.wait_ge(delta_spread, UNITS * (b - 1))
                        for q in range(2):
                            rows = slice(64 * q, 64 * q + 64)
                            act.activation((delta_h, du_h)[step[2]][rows, b % 2, q], src[rows], ACT.Copy).then_inc(done, 1)
                    else:
                        if b >= 2:
                            act.wait_ge(du_moved, 64 * (b - 1))
                        act.activation(du_parts[:, 0], src[:], ACT.Copy).then_inc(done, 1)
                elif kind == "tables":
                    act.wait_ge(project_ready, 3)
                    act.activation(a_neg[:], a_exp[:], ACT.Exp).then_inc(a_raw, 1)
                    act.wait_ge(a_raw, 1)
                    act.activation(a_exp[:], a_neg[:], ACT.Copy, scale=-1.0).then_inc(a_raw, 1)
                    act.wait_ge(a_raw, 2)
                    act.activation(a_neg[:], a_exp[:], ACT.Copy).then_inc(a_ready, 1)
                    act.wait_ge(a_ready, 1)
                elif kind == "ahead":
                    for n in range(SPREAD_AHEAD - 1):
                        decay_of(n)
                elif kind == "unit":
                    n = index(*step[1:]) + SPREAD_AHEAD - 1
                    if n < UNITS * B:
                        decay_of(n)
                elif kind == "split_up":
                    k, w = divmod(step[1], 2)
                    act.wait_ge(up_loaded, 32)
                    act.activation(up_hi[:, k, w], up_raw[:, k, w].rearrange("p (g j) -> p j g", j=4),
                                   ACT.Copy).then_inc(hi_ready, 1)
                elif kind == "norm":
                    act.preload_act_table_set("silu_and_others")
                elif kind == "normed":
                    bank = has(act, step)
                    if b:
                        has(act, ("up", b - 1, 3))
                    act.activation(xnt_hi[:], bank[:], ACT.Copy).then_inc(xnt_hi_ready, 1)
                elif kind == "gate":
                    i = step[2]
                    bank = has(act, step)
                    if b:
                        act.wait_ge(h_ready, 4 * (b - 1) + i + 1)
                    last = b == B - 1
                    act.activation(gate_s[:, i // 2, 2 * (i % 2):2 * (i % 2) + 2], bank[:],
                                   ACT.Silu if last else ACT.Copy).then_inc(gate_ready if last else gate_out, 1)
                elif kind == "silu":
                    act.preload_act_table_set("silu_and_others")
                    if b + 2 < B:
                        act.wait_ge(mixed_ready, C * (b + 1))
                        z_gate_of(b + 2)
                    for i in range(4):
                        act.wait_ge(gate_out, 4 * b + i + 1)
                        act.activation(gate_s[:, i // 2, 2 * (i % 2):2 * (i % 2) + 2],
                                       gate_s[:, i // 2, 2 * (i % 2):2 * (i % 2) + 2], ACT.Silu).then_inc(gate_ready, 1)
                    act.preload_act_table_set("natural_log_exp_and_others")
                elif kind == "compare":
                    c = step[2]
                    act.wait_ge(h_ready, 4 * b + 2 * c + 2)
                    if b:
                        act.wait_ge(beats_ready, 3 * (2 * (b - 1) + c + 1))
                    act.activation(h_abs[:, c], h[:, c], ACT.Abs).then_inc(h_abs_ready, 1)

        @block.vector
        def _(dve):
            def drive_of(n):
                b = n // UNITS
                dve.wait_ge(du_spread, n + 1)
                dve.wait_ge(bc_ready, b + 1)
                if n >= N_DRIVE:
                    dve.wait_ge(scanned, n - N_DRIVE + 1)
                dve.tensor_tensor(drive[:, n % N_DRIVE], drv_ps[n % 2][:], bc[:, b % 2, 0:1].broadcast_to([P, 2, L]),
                                  ALU.mult).then_inc(drive_ready, 1)

            for step in steps_of(V):
                kind, b = step[0], step[1] if len(step) > 1 else None
                if kind == "taps":
                    dve.wait_ge(taps_loaded, 32)
                    bank = has(dve, ("taps", 0))
                    rows = tap_rows.rearrange("p j (e k) -> p j e k", k=TAPS)
                    for k in range(TAPS):
                        dve.tensor_tensor(in_taps[:, k].rearrange("p (j e) -> p j e", j=4),
                                          bank[:, 0].rearrange("p (j e) -> p j e", j=4), rows[:, :, :, k],
                                          ALU.mult).then_inc(taps_ready, 1)
                elif kind == "project":
                    bank = has(dve, ("project", 0))
                    W = DR + 2 * NS
                    dve.tensor_copy(xproj_t[:, :, 0:2 * NS], bank[:, :, DR:W])
                    dve.tensor_copy(xproj_t[:, :, 2 * NS:W], bank[:, :, 0:DR]).then_inc(project_ready, 1)
                    bank = has(dve, ("project", 1))
                    dve.tensor_copy(step_wt[:], bank[0:DR].rearrange("p a t -> p (a t)")[:, 0:D_IN]).then_inc(project_ready, 1)
                elif kind == "context":
                    dve.wait_ge(x_loaded[b], 16)
                    for c in range(C):
                        dve.bn_stats(stats[:, b, c], x_sb[:, b, c]).then_inc(x_stats, 1)
                    for c in range(C):
                        dve.wait_ge(x_stats, C * b + c + 1)
                        dve.bn_aggr(moments[:, b, c], stats[:, b, c]).then_inc(x_moments, 1)
                    dve.wait_ge(x_moments, C * (b + 1))
                    dve.tensor_scalar(veps[:, b], moments[:, b, :, 1], EPS, None, ALU.add).then_inc(x_veps, 1)
                elif kind == "shift":
                    dve.wait_ge(x_rstd, b + 1)
                    dve.scalar_tensor_tensor(shift[:, b], moments[:, b, :, 0], -1.0, rstd[:, b], ALU.mult,
                                             ALU.mult).then_inc(x_shift, 1)
                elif kind == "x_dbl":
                    bank = has(dve, step)
                    dve.tensor_copy(low[:, b % 2], bank[2 * NS:2 * NS + DR, 0]).then_inc(low_ready, 1)
                    if b:
                        dve.wait_ge(bc_ready, b)
                    dve.tensor_copy(bc_parts[0:2 * NS], bank[0:2 * NS, 0]).then_inc(bc_hi, 1)
                    dve.wait_ge(bc_hi, b + 1)
                    dve.tensor_tensor(bc_parts[2 * NS:4 * NS], bank[0:2 * NS, 0], bc_parts[0:2 * NS].bitcast(F32),
                                      ALU.subtract).then_inc(bc_lo, 1)
                elif kind == "split_up" and step[1] % 2:
                    k, w = divmod(step[1], 2)
                    dve.wait_ge(hi_ready, step[1] + 1)
                    dve.tensor_tensor(up_lo[:, k, w], up_raw[:, k, w].rearrange("p (g j) -> p j g", j=4),
                                      up_hi[:, k, w].bitcast(F32), ALU.subtract).then_inc(lo_ready, 1)
                elif kind == "softplus":
                    if b == 0:
                        bank = has(dve, ("step", 0))
                        dve.wait_ge(abs_ready, 1)
                        for c in range(C):
                            last = dve.tensor_scalar(sp_pos[:, c], bank[:, c], step_b_sb[:, c:c + 1], 0.0, ALU.add, ALU.max)
                        last.then_inc(pos_ready, 1)
                    dve.wait_ge(exp_ready, b + 1)
                    dve.tensor_scalar(sp_back[:], sp_exp[:], 1.0, 1.0, ALU.add, ALU.subtract).then_inc(back_ready, 1)
                    dve.wait_ge(back_ready, b + 1)
                    if b:
                        dve.wait_ge(sum_ready, b)
                    dve.tensor_tensor(sp_lost[:], sp_exp[:], sp_back[:], ALU.subtract).then_inc(lost_ready, 1)
                    if b == 0:
                        dve.wait_ge(lost_ready, 1)
                        dve.wait_ge(pos_ready, 1)
                        dve.tensor_tensor(sp_abs[:], sp_pos[:], sp_lost[:], ALU.add).then_inc(sum_ready, 1)
                elif kind == "delta" and b == 0:
                    dve.wait_ge(ln_ready, b + 1)
                    dve.wait_ge(sum_ready, b + 1)
                    dve.tensor_tensor(delta[:], sp_abs[:], sp_ln[:], ALU.add).then_inc(delta_ready, 1)
                    dve.wait_ge(delta_ready, 1)
                    dve.tensor_tensor(du[:], delta[:], u[:, 0], ALU.mult).then_inc(du_ready, 1)
                elif kind == "halves":
                    if b == 0:
                        for src, dst, hi, done, q in ((delta, delta_h, delta_hi, delta_lo, 0), (du, du_h, du_hi, du_lo, 0),
                                                      (du, du_h, du_hi, du_lo, 1)):
                            lower_half(dve, src, dst, 0, q, hi, 2 * b + q + 1, done)
                        continue
                    src, hi, done = ((delta, delta_hi, delta_lo), (du, du_hi, du_lo))[step[2]]
                    if direct(*step[1:]):
                        dst = (delta_h, du_h)[step[2]]
                        for q in range(2):
                            lower_half(dve, src, dst, b % 2, q, hi, 2 * b + q + 1, done)
                    else:
                        dve.wait_ge(hi, b + 2)
                        dve.tensor_tensor(du_parts[:, 1], src[:], du_parts[:, 0].bitcast(F32), ALU.subtract).then_inc(done, 1)
                elif kind == "unit":
                    n = index(*step[1:])
                    if n + 1 < UNITS * B:
                        drive_of(n + 1)
                    dve.wait_ge(drive_ready, n + 1)
                    dve.wait_ge(decay_ready, n + 1)
                    if n >= N_STATE:
                        dve.wait_ge(prod_ready, n - N_STATE + 1)
                    dve.tensor_tensor_scan(state[:, n % N_STATE].rearrange("p a t -> p (a t)"),
                                           decay[:, n % N_DECAY].rearrange("p a t -> p (a t)"),
                                           drive[:, n % N_DRIVE].rearrange("p a t -> p (a t)"), 0.0, ALU.mult,
                                           ALU.add).then_inc(scanned, 1)
                elif kind == "ahead":
                    drive_of(0)
                elif kind == "finish":
                    c = step[2]
                    n = C * b + c
                    dve.wait_ge(summed, UNITS // 2 // C * (n + 1))
                    dve.wait_ge(u_ready, b + 1)
                    if b:
                        has(dve, ("residual", b - 1))
                    dve.scalar_tensor_tensor(mixed[:, c], u[:, b % 3, c], skip_sb[:, c:c + 1], y_ps[:, c], ALU.mult,
                                             ALU.add).then_inc(skip_added, 1)
                elif kind == "residual":
                    bank = has(dve, step)
                    dve.wait_ge(gains_ready, 1)
                    dve.wait_ge(x_loaded[b], 16)
                    for c in range(C):
                        last = dve.scalar_tensor_tensor(x2[:, b, c], bank[:, c], gains[:, 0:1], x_sb[:, b, c],
                                                        ALU.mult, ALU.add)
                        last.then_inc(x2_ready, 1)
                    dve.wait_ge(x2_ready, C * (b + 1))
                    for c in range(C):
                        dve.bn_stats(stats2[:, b, c], x2[:, b, c]).then_inc(s_stats, 1)
                    for c in range(C):
                        dve.wait_ge(s_stats, C * b + c + 1)
                        dve.bn_aggr(moments2[:, b, c], stats2[:, b, c]).then_inc(s_moments, 1)
                    dve.wait_ge(s_moments, C * (b + 1))
                    dve.tensor_scalar(veps2[:, b], moments2[:, b, :, 1], EPS, None, ALU.add).then_inc(s_veps, 1)
                elif kind == "norm":
                    dve.wait_ge(s_rstd, b + 1)
                    if b:
                        has(dve, ("normed", b - 1))
                    for c in range(C):
                        dve.tensor_scalar(xn[:, c], x2[:, b, c], moments2[:, b, c, 0:1], rstd2[:, b, c:c + 1],
                                          ALU.subtract, ALU.mult).then_inc(xn_ready, 1)
                elif kind == "normed":
                    bank = has(dve, step)
                    dve.wait_ge(xnt_hi_ready, b + 1)
                    dve.tensor_tensor(xnt_lo[:], bank[:], xnt_hi[:].bitcast(F32), ALU.subtract).then_inc(xnt_lo_ready, 1)
                elif kind == "up":
                    i = step[2]
                    bank = has(dve, step)
                    dve.wait_ge(gate_ready, 4 * b + i + 1)
                    if b:
                        dve.wait_ge(kept_ready, 8 * (b - 1) + 4 * (i // 2) + 4)
                        dve.wait_ge(h_abs_ready, 2 * (b - 1) + i // 2 + 1)
                    mem = slice(2 * (i % 2), 2 * (i % 2) + 2)
                    dve.tensor_tensor(h[:, i // 2, mem], gate_s[:, i // 2, mem], bank[:], ALU.mult).then_inc(h_ready, 1)
                elif kind == "compare":
                    c = step[2]
                    n = 2 * b + c
                    dve.wait_ge(h_abs_ready, n + 1)
                    if b:
                        has(dve, ("wins", b - 1, c, 1))
                    for at, m, d in ((0, 3, 1), (3, 2, 2), (5, 1, 3)):
                        dve.tensor_tensor(beats[:, c, at:at + m], h_abs[:, c, 0:m], h_abs[:, c, d:d + m],
                                          ALU.is_ge).then_inc(beats_ready, 1)
                elif kind == "wins":
                    _, _, c, pair = step
                    bank = has(dve, step)
                    dve.wait_ge(h_ready, 4 * b + 2 * c + 2)
                    if b:
                        for key in [("down", b - 1)] if b - 1 < B - 2 else [("down", b - 1, tt) for tt in range(2)]:
                            has(dve, key)
                    for m in range(2):
                        j = 2 * pair + m
                        last = dve.scalar_tensor_tensor(h_kept[:, c, j], bank[:, m], 1.5 - j, h[:, c, j],
                                                        ALU.is_ge, ALU.mult)
                        last.then_inc(kept_ready, 1)
                elif kind == "result":
                    tt = step[2]
                    bank = has(dve, ("down", b) if tt is None else ("down", b, tt))
                    if tt is None:
                        dve.scalar_tensor_tensor(x2[:, b], bank[:], gains[:, 1:2], x2[:, b], ALU.mult,
                                                 ALU.add).then_inc(result_ready, C)
                    else:
                        dve.scalar_tensor_tensor(x2[:, b, tt], bank[:, 0], gains[:, 1:2], x2[:, b, tt], ALU.mult,
                                                 ALU.add).then_inc(result_ready, 1)

        @block.tensor
        def _(pe):
            def take(key):
                n, _, prior = BANK[key]
                if prior:
                    pe.wait_ge(*last_read(prior))
                return work[n]

            def spread(n, src, dst, ready):
                b, k = divmod(n, UNITS)
                c = k // (UNITS // C)
                for half in range(2):
                    g, quad = group(k, half)
                    last = pe.matmul(dst[n % 2][:, half], spread_r[:, g % ES], src[:, b % 2, quad // 2, c],
                                     start=True, stop=True)
                last.then_inc(ready, 1)

            def spread_delta(n):
                if n % UNITS == 0 or n == 1:
                    pe.wait_ge(delta_hi, n + 1 if n < 2 else 2 * (n // UNITS + 1))
                    if n == 1:
                        pe.wait_ge(delta_lo_1, 1)
                    else:
                        pe.wait_ge(delta_lo, 2 * (n // UNITS) + 1)
                if n >= 2:
                    pe.wait_ge(decay_ready, n - 1)
                spread(n, delta_h, dec_ps, delta_spread)

            def spread_du(n):
                if n % UNITS == 0:
                    if n:
                        pe.wait_ge(du_moved, 64 * (n // UNITS))
                if n < 2:
                    pe.wait_ge(du_hi, n + 1)
                    pe.wait_ge(du_lo, n + 1)
                if n >= 2:
                    pe.wait_ge(drive_ready, n - 1)
                spread(n, du_h, drv_ps, du_spread)

            def sum_states(s):
                b, r = divmod(s, UNITS // 2)
                c, r = divmod(r, SETS)
                pe.wait_ge(prod_ready, 2 * s + 2)
                if s == 0:
                    pe.wait_ge(u_ready, 2)
                if r == 0 and s >= SETS:
                    pe.wait_ge(skip_added, C * b + c)
                for quad in range(QUADS):
                    n = 2 * s + quad // 2
                    last = pe.matmul(y_ps[32 * quad:32 * quad + 32, c], gather[:, r], prod[:, n % N_PROD, quad % 2],
                                     start=(r == 0), stop=(r == SETS - 1), tile_position=(0, 32 * quad))
                last.then_inc(summed, 1)

            for step in steps_of(T):
                kind, b = step[0], step[1] if len(step) > 1 else None
                if kind == "load":
                    pe.wait_ge(warm_ready, 1)
                    for _ in range(WARM):
                        pe.matmul(work[0][:, 0, 0:P], warm[:], warm[:], start=True, stop=True)
                elif kind == "taps":
                    pe.wait_ge(taps_loaded, 32)
                    pe.wait_ge(masks_ready, 1)
                    bank = take(("taps", 0))
                    for c in range(C):
                        last = pe.transpose(bank[:, 0, c * P:(c + 1) * P], in_w_sb[:, c], ident[:])
                    last.then_inc(filled[0], 1)
                elif kind == "project":
                    pe.wait_ge(proj_loaded, 16 * 3)
                    bank = take(("project", 0))
                    W = DR + 2 * NS
                    for c in range(C):
                        last = pe.transpose(bank[:, c, 0:W], xproj_sb[:, c * P:(c + 1) * P], ident[0:W, 0:W])
                    last.then_inc(filled[BANK["project", 0][0]], 1)
                    bank = take(("project", 1))
                    for c in range(C):
                        last = pe.transpose(bank[0:DR, 0, c * P:(c + 1) * P], step_w_sb[:, c], ident[:])
                    last.then_inc(filled[BANK["project", 1][0]], 1)
                    bank = take(("project", 2))
                    pe.transpose(bank[:, 0, 0:GROUPS], a_log_sb[:], ident[0:GROUPS, 0:GROUPS]).then_inc(
                        filled[BANK["project", 2][0]], 1)
                elif kind == "context":
                    pe.wait_ge(ctx_loaded[b], 16)
                    if b == 0:
                        pe.wait_ge(masks_ready, 1)
                    bank = take(step)
                    for c in range(C):
                        last = pe.transpose(bank[:, 0, c * P:(c + 1) * P], ctx_sb[:, b, c], ident[:])
                    last.then_inc(filled[BANK[step][0]], 1)
                elif kind == "conv":
                    q = step[2]
                    c = q // 2
                    if q == 0:
                        take(("conv", b))
                        pe.wait_ge(ctx_turned, b + 1)
                        pe.wait_ge(pads_ready, 1)
                    bank = work[BANK["conv", b][0]]
                    for k in range(2 * (q % 2), 2 * (q % 2) + 2):
                        if b == 0 and q < 2:
                            pe.wait_ge(taps_ready, k + 1)
                        last = pe.matmul(bank[:, c], in_taps[:, k, c * P:(c + 1) * P], ctx_t[:, b % 2, k:k + L],
                                         start=(k == 0), stop=(k == TAPS - 1))
                    if q == 3:
                        last.then_inc(filled[BANK["conv", b][0]], 1)
                elif kind == "x_dbl":
                    pe.wait_ge(u_ready, b + 1)
                    if b == 0:
                        pe.wait_ge(project_ready, 2)
                    bank = take(step)
                    for c in range(C):
                        last = pe.matmul(bank[0:2 * NS + DR, 0], xproj_t[:, c], u[:, b % 3, c], start=(c == 0), stop=(c == C - 1))
                    last.then_inc(filled[BANK[step][0]], 1)
                elif kind == "bc":
                    pe.wait_ge(bc_hi, b + 1)
                    pe.wait_ge(bc_lo, b + 1)
                    if b == 0:
                        pe.wait_ge(masks_cast, 2)
                    bank = take(step)
                    for i in range(2):
                        last = pe.matmul(bank[:, i], spread_bc[:, i], bc_parts[:], start=True, stop=True)
                    last.then_inc(filled[BANK[step][0]], 1)
                elif kind == "step":
                    pe.wait_ge(low_ready, b + 1)
                    bank = take(step)
                    for c in range(C):
                        last = pe.matmul(bank[:, c], step_wt[:, c * P:(c + 1) * P], low[:, b % 2], start=True, stop=True)
                    last.then_inc(filled[2], 1)
                elif kind == "ahead":
                    pe.wait_ge(masks_cast, 4)
                    for n in range(SPREAD_AHEAD):
                        spread_delta(n)
                        if n == 0:
                            spread_du(0)
                            spread_du(1)
                elif kind == "unit":
                    n = index(*step[1:])
                    if n + 2 < UNITS * B:
                        spread_du(n + 2)
                    first = spread_by(n - 1, WINDOWS) + 1 if n else SPREAD_AHEAD
                    for m in range(first, spread_by(n, WINDOWS) + 1):
                        spread_delta(m)
                    if n % 2 == 0 and n >= 4:
                        sum_states(n // 2 - 2)
                elif kind == "flush":
                    for s in range(UNITS * B // 2 - 2, UNITS * B // 2):
                        sum_states(s)
                elif kind == "residual":
                    pe.wait_ge(mixed_ready, C * (b + 1))
                    bank = take(step)
                    for lt in range(C):
                        for c in range(C):
                            last = pe.transpose(bank[:, lt, c * P:(c + 1) * P], mixed[:, c, lt * P:(lt + 1) * P], ident[:])
                    last.then_inc(filled[BANK[step][0]], 1)
                elif kind == "normed":
                    pe.wait_ge(xn_ready, C * (b + 1))
                    bank = take(step)
                    for k in range(KB):
                        for lt in range(C):
                            last = pe.transpose(bank[:, k, lt * P:(lt + 1) * P], xn[:, lt, k * P:(k + 1) * P], ident[:])
                    last.then_inc(filled[BANK[step][0]], 1)
                elif kind in ("gate", "up"):
                    i, w = step[2], 0 if kind == "gate" else 1
                    if i == 0 and w == 0:
                        pe.wait_ge(xnt_hi_ready, b + 1)
                        pe.wait_ge(xnt_lo_ready, b + 1)
                        if b == 0:
                            pe.wait_ge(hi_ready, 4)
                            pe.wait_ge(lo_ready, 4)
                    bank = take(step)
                    for m in range(2):
                        j = 2 * (i % 2) + m
                        cols = slice((i // 2) * P, (i // 2 + 1) * P)
                        terms = [(a, x_, k) for k in range(KB) for a, x_ in ((up_hi, xnt_lo), (up_lo, xnt_hi), (up_hi, xnt_hi))]
                        for t, (a, x_, k) in enumerate(terms):
                            last = pe.matmul(bank[:, m], a[:, k, w, j, cols], x_[:, k], start=(t == 0),
                                             stop=(t == len(terms) - 1))
                    last.then_inc(filled[BANK[step][0]], 1)
                elif kind == "wins":
                    _, _, c, pair = step
                    pe.wait_ge(beats_ready, 3 * (2 * b + c + 1))
                    bank = take(step)
                    terms = (((plus_b, 0), (plus_b, 3), (plus_b, 5)), ((minus_b, 0), (plus_b, 1), (plus_b, 4)),
                             ((minus_b, 3), (minus_b, 1), (plus_b, 2)), ((minus_b, 5), (minus_b, 4), (minus_b, 2)))
                    for m in range(2):
                        for t, (sign, at) in enumerate(terms[2 * pair + m]):
                            last = pe.matmul(bank[:, m], sign[:], beats[:, c, at], start=(t == 0), stop=(t == 2))
                    last.then_inc(filled[BANK[step][0]], 1)
                elif kind == "down":
                    _, _, tt, c = step
                    one = b < B - 2
                    key = step[:2] if one else step[:3]
                    if c == 0 and not (one and tt):
                        take(key)
                        if b == 0:
                            pe.wait_ge(down_loaded, 16)
                    bank = work[BANK[key][0]]
                    for j in range(4):
                        pe.wait_ge(kept_ready, 8 * b + 4 * c + j + 1)
                        last = pe.matmul(bank[:, tt if one else 0], h_kept[:, c, j, tt * P:(tt + 1) * P], down_sb[:, c, j],
                                         start=(c == 0 and j == 0), stop=(c == IC - 1 and j == 3))
                    if c == IC - 1 and (tt or not one):
                        last.then_inc(filled[BANK[key][0]], 1)


_INS = ['x', 'ctx_1024', 'g_xattn', 'g_ffn', 'L0_xattn_in_proj_w', 'L0_xattn_conv_w', 'L0_xattn_conv_b',
        'L0_xattn_x_proj_w', 'L0_xattn_dt_proj_w', 'L0_xattn_dt_proj_b', 'L0_xattn_A_log', 'L0_xattn_D',
        'L0_ffn_w_gate', 'L0_ffn_w_up', 'L0_ffn_w_down']


def kernel(**inputs):
    import numpy as _np
    import concourse.bacc as _bacc
    from concourse.bass_utils import run_bass_kernel_spmd as _run

    nc = _bacc.Bacc("TRN2", target_bir_lowering=False, num_devices=1)
    arrays, args = {}, []
    for name in _INS:
        a = _np.ascontiguousarray(inputs[name])
        arrays[f"in_{name}_dram"] = a
        args.append(nc.dram_tensor(f"in_{name}_dram", a.shape, mybir.dt.from_np(a.dtype), kind="ExternalInput").ap())
    args.append(nc.dram_tensor("out_dram", (B, L, D_IN), mybir.dt.float32, kind="ExternalOutput").ap())
    gated_block(nc, *args)
    r = _run(nc, [arrays], core_ids=[0])
    return r.results[0]["out_dram"]
```
